# Optimizing a Trainium2 kernel written in Bass

```python
import numpy as np
import jax
import jax.numpy as jnp

def _softmax(x, axis=-1):
    return jax.nn.softmax(x, axis=axis)

def _gelu(x):
    return jax.nn.gelu(x, approximate=True)

def _silu(x):
    return jax.nn.silu(x)

def _sigmoid(x):
    return jax.nn.sigmoid(x)

def _layernorm(x, axis=-1, eps=1e-05):
    m = jnp.mean(x, axis=axis, keepdims=True)
    v = jnp.var(x, axis=axis, keepdims=True)
    return (x - m) / jnp.sqrt(v + eps)

def _scatter_add(tgt, idx, src, axis=0):
    return tgt.at[idx].add(src)

def _segment_sum(src, seg, n):
    return jax.ops.segment_sum(src, seg, n)
kernel_name = 'mk_gps_d1_gnn_r8_ccc980'

def setup_inputs(seed: int=0):
    np.random.seed(seed)
    _w = jnp.asarray

    def _rec_inputs():
        import jax
        import jax.numpy as jnp
        _gk = jax.random.key(seed)
        x = -0.0003713 + 1 * jax.random.normal(jax.random.fold_in(_gk, 1), (6250, 256), jnp.float32)
        src = jax.random.randint(jax.random.fold_in(_gk, 2), (200000,), 0, 6250, jnp.int32)
        dst = jnp.minimum((6250 * jax.random.uniform(jax.random.fold_in(_gk, 3), (200000,)) ** 2.0).astype(jnp.int32), 49999)
        _o = jnp.argsort(dst, stable=True)
        src = src[_o]
        dst = dst[_o]
        return (x, src, dst)
    x, src, dst = _rec_inputs()

    def _L0_gnn_setup():
        import jax, jax.numpy as jnp
        import numpy as np
        N_NODES = 6250
        N_EDGES = 100000
        IN_DIM = 256
        N_HEADS = 4
        HEAD_DIM = 64
        NEG_SLOPE = 0.2

        def _gat_conv(x, edge_index, W, att_src, att_dst):
            n = x.shape[0]
            loops = jnp.arange(n, dtype=edge_index.dtype)
            src = jnp.concatenate([edge_index[0], loops])
            dst = jnp.concatenate([edge_index[1], loops])
            xp = (x @ W).reshape(n, N_HEADS, HEAD_DIM)
            a_src = jnp.einsum('nhc,hc->nh', xp, att_src)
            a_dst = jnp.einsum('nhc,hc->nh', xp, att_dst)
            e = jax.nn.leaky_relu(a_src[src] + a_dst[dst], NEG_SLOPE)
            e_max = jax.ops.segment_max(e, dst, num_segments=n)
            e_exp = jnp.exp(e - e_max[dst])
            denom = jax.ops.segment_sum(e_exp, dst, num_segments=n)
            alpha = e_exp / denom[dst]
            out = jax.ops.segment_sum(alpha[:, :, None] * xp[src], dst, num_segments=n)
            return out.reshape(n, N_HEADS * HEAD_DIM)
        key = jax.random.key(seed)
        k1, k2, k3, k4, k5 = jax.random.split(key, 5)
        x = jax.random.normal(k1, (N_NODES, IN_DIM), dtype=jnp.float32)
        edge_index = jax.random.randint(k2, (2, N_EDGES), 0, N_NODES, dtype=jnp.int64)
        w_scale = (2.0 / (IN_DIM + N_HEADS * HEAD_DIM)) ** 0.5
        W = jax.random.normal(k3, (IN_DIM, N_HEADS * HEAD_DIM), dtype=jnp.float32) * w_scale
        a_scale = (2.0 / (1 + HEAD_DIM)) ** 0.5
        att_src = jax.random.normal(k4, (N_HEADS, HEAD_DIM), dtype=jnp.float32) * a_scale
        att_dst = jax.random.normal(k5, (N_HEADS, HEAD_DIM), dtype=jnp.float32) * a_scale
        return {'x': x, 'edge_index': edge_index, 'W': W, 'att_src': att_src, 'att_dst': att_dst}
    _L0_gnn_all = _L0_gnn_setup()
    _L0_gnn_in = {k: v for k, v in _L0_gnn_all.items() if k in ('W', 'att_src', 'att_dst')}
    del _L0_gnn_all

    def _L0_mix_setup():
        import math
        import jax, jax.numpy as jnp
        import numpy as np
        EPS_DIV = 1e-07
        EPS_NORM = 1e-12

        def _l2_normalize(x, axis):
            n = jnp.sqrt(jnp.sum(x * x, axis=axis, keepdims=True))
            return x / jnp.maximum(n, EPS_NORM)
        key = jax.random.key(seed)
        ks = jax.random.split(key, 5)
        b, N, C = (8, 512, 256)
        x = jax.random.normal(ks[0], (b, N, C), dtype=jnp.float32)
        W_qkv = jax.random.normal(ks[1], (C, 3 * C), dtype=jnp.float32) * (1.0 / math.sqrt(C))
        b_qkv = jax.random.normal(ks[2], (3 * C,), dtype=jnp.float32) * 0.02
        W_out = jax.random.normal(ks[3], (C, C), dtype=jnp.float32) * (1.0 / math.sqrt(C))
        b_out = jax.random.normal(ks[4], (C,), dtype=jnp.float32) * 0.02
        return {'x': x, 'W_qkv': W_qkv, 'b_qkv': b_qkv, 'W_out': W_out, 'b_out': b_out}
    _L0_mix_all = _L0_mix_setup()
    _L0_mix_in = {k: v for k, v in _L0_mix_all.items() if k in ('W_qkv', 'b_qkv', 'W_out', 'b_out')}
    del _L0_mix_all

    def _L0_ffn_setup():
        import jax, jax.numpy as jnp
        import numpy as np
        BN_EPS = 0.001

        def _bn(h, g, b, m, v):
            return g * (h - m) * jax.lax.rsqrt(v + BN_EPS) + b
        key = jax.random.key(seed)
        ks = jax.random.split(key, 8)
        B, F, Df = (256, 64, 256)
        E, H, D = (8, 256, 256)
        s1 = 1.0 / np.sqrt(Df)
        s2 = 1.0 / np.sqrt(H)
        return {'x': jax.random.normal(ks[0], (B, F, Df), jnp.float32), 'Wr': jax.random.normal(ks[1], (Df, E), jnp.float32) * s1, 'br': jnp.zeros((E,), jnp.float32), 'W1': jax.random.normal(ks[2], (E, Df, H), jnp.float32) * s1, 'b1': jnp.zeros((E, H), jnp.float32), 'g1': jnp.ones((E, H), jnp.float32), 'be1': jnp.zeros((E, H), jnp.float32), 'm1': jnp.zeros((E, H), jnp.float32), 'v1': jnp.ones((E, H), jnp.float32), 'W2': jax.random.normal(ks[3], (E, H, H), jnp.float32) * s2, 'b2': jnp.zeros((E, H), jnp.float32), 'g2': jnp.ones((E, H), jnp.float32), 'be2': jnp.zeros((E, H), jnp.float32), 'm2': jnp.zeros((E, H), jnp.float32), 'v2': jnp.ones((E, H), jnp.float32), 'Wo': jax.random.normal(ks[4], (E, H, D), jnp.float32) * s2, 'bo': jnp.zeros((E, D), jnp.float32)}
    _L0_ffn_all = _L0_ffn_setup()
    _L0_ffn_in = {k: v for k, v in _L0_ffn_all.items() if k in ('Wr', 'br', 'W1', 'b1', 'g1', 'be1', 'm1', 'v1', 'W2', 'b2', 'g2', 'be2', 'm2', 'v2', 'Wo', 'bo')}
    del _L0_ffn_all
    return {'x': x, 'src': src, 'dst': dst, 'L0_gnn_W': _L0_gnn_in['W'], 'L0_gnn_att_src': _L0_gnn_in['att_src'], 'L0_gnn_att_dst': _L0_gnn_in['att_dst'], 'L0_mix_W_qkv': _L0_mix_in['W_qkv'], 'L0_mix_b_qkv': _L0_mix_in['b_qkv'], 'L0_mix_W_out': _L0_mix_in['W_out'], 'L0_mix_b_out': _L0_mix_in['b_out'], 'L0_ffn_Wr': _L0_ffn_in['Wr'], 'L0_ffn_br': _L0_ffn_in['br'], 'L0_ffn_W1': _L0_ffn_in['W1'], 'L0_ffn_b1': _L0_ffn_in['b1'], 'L0_ffn_g1': _L0_ffn_in['g1'], 'L0_ffn_be1': _L0_ffn_in['be1'], 'L0_ffn_m1': _L0_ffn_in['m1'], 'L0_ffn_v1': _L0_ffn_in['v1'], 'L0_ffn_W2': _L0_ffn_in['W2'], 'L0_ffn_b2': _L0_ffn_in['b2'], 'L0_ffn_g2': _L0_ffn_in['g2'], 'L0_ffn_be2': _L0_ffn_in['be2'], 'L0_ffn_m2': _L0_ffn_in['m2'], 'L0_ffn_v2': _L0_ffn_in['v2'], 'L0_ffn_Wo': _L0_ffn_in['Wo'], 'L0_ffn_bo': _L0_ffn_in['bo']}

def reference(x, src, dst, L0_gnn_W, L0_gnn_att_src, L0_gnn_att_dst, L0_mix_W_qkv, L0_mix_b_qkv, L0_mix_W_out, L0_mix_b_out, L0_ffn_Wr, L0_ffn_br, L0_ffn_W1, L0_ffn_b1, L0_ffn_g1, L0_ffn_be1, L0_ffn_m1, L0_ffn_v1, L0_ffn_W2, L0_ffn_b2, L0_ffn_g2, L0_ffn_be2, L0_ffn_m2, L0_ffn_v2, L0_ffn_Wo, L0_ffn_bo):
    import jax
    import jax.numpy as jnp

    def _L0_gnn_ref(x, edge_index, W, att_src, att_dst):
        import jax, jax.numpy as jnp
        import numpy as np
        N_NODES = 6250
        N_EDGES = 100000
        IN_DIM = 256
        N_HEADS = 4
        HEAD_DIM = 64
        NEG_SLOPE = 0.2

        def _gat_conv(x, edge_index, W, att_src, att_dst):
            n = x.shape[0]
            loops = jnp.arange(n, dtype=edge_index.dtype)
            src = jnp.concatenate([edge_index[0], loops])
            dst = jnp.concatenate([edge_index[1], loops])
            xp = (x @ W).reshape(n, N_HEADS, HEAD_DIM)
            a_src = jnp.einsum('nhc,hc->nh', xp, att_src)
            a_dst = jnp.einsum('nhc,hc->nh', xp, att_dst)
            e = jax.nn.leaky_relu(a_src[src] + a_dst[dst], NEG_SLOPE)
            e_max = jax.ops.segment_max(e, dst, num_segments=n)
            e_exp = jnp.exp(e - e_max[dst])
            denom = jax.ops.segment_sum(e_exp, dst, num_segments=n)
            alpha = e_exp / denom[dst]
            out = jax.ops.segment_sum(alpha[:, :, None] * xp[src], dst, num_segments=n)
            return out.reshape(n, N_HEADS * HEAD_DIM)
        y = _gat_conv(x, edge_index, W, att_src, att_dst)
        return jax.nn.relu(y)

    def _L0_mix_ref(x, W_qkv, b_qkv, W_out, b_out):
        import math
        import jax, jax.numpy as jnp
        import numpy as np
        EPS_DIV = 1e-07
        EPS_NORM = 1e-12

        def _l2_normalize(x, axis):
            n = jnp.sqrt(jnp.sum(x * x, axis=axis, keepdims=True))
            return x / jnp.maximum(n, EPS_NORM)
        b, N, C = x.shape
        qkv = x @ W_qkv + b_qkv
        q, k, v = jnp.split(qkv, 3, axis=2)
        q = q - jnp.mean(q, axis=2, keepdims=True)
        k = k - jnp.mean(k, axis=2, keepdims=True)
        q2 = q * q
        k2 = k * k
        q2s = jnp.sum(q2, axis=2, keepdims=True)
        k2s = jnp.sum(k2, axis=2, keepdims=True)
        k2 = _l2_normalize(k2 / (k2s + EPS_DIV), axis=-2)
        q2 = _l2_normalize(q2 / (q2s + EPS_DIV), axis=-1)
        kv = jnp.einsum('bnc,bnd->bcd', k2, v)
        t2 = jnp.einsum('bnc,bcd->bnd', q2, kv) / math.sqrt(N)
        attn = v + t2
        return attn @ W_out + b_out

    def _L0_ffn_ref(x, Wr, br, W1, b1, g1, be1, m1, v1, W2, b2, g2, be2, m2, v2, Wo, bo):
        import jax, jax.numpy as jnp
        import numpy as np
        BN_EPS = 0.001

        def _bn(h, g, b, m, v):
            return g * (h - m) * jax.lax.rsqrt(v + BN_EPS) + b
        feat = jnp.mean(x, axis=0)
        w = jax.nn.softmax(feat @ Wr + br, axis=-1)
        h = jnp.einsum('bfd,edh->bfeh', x, W1) + b1
        h = jax.nn.relu(_bn(h, g1, be1, m1, v1))
        h = jnp.einsum('bfeh,ehk->bfek', h, W2) + b2
        h = jax.nn.relu(_bn(h, g2, be2, m2, v2))
        y = jnp.einsum('bfeh,ehd->bfed', h, Wo) + bo
        return jnp.einsum('bfed,fe->bfd', y, w)
    edge_index = jnp.stack([src, dst])
    xn = _layernorm(x, axis=-1)
    x = x + _L0_gnn_ref(xn, edge_index, L0_gnn_W, L0_gnn_att_src, L0_gnn_att_dst) + _L0_mix_ref(xn[None], L0_mix_W_qkv, L0_mix_b_qkv, L0_mix_W_out, L0_mix_b_out)[0]
    x = x + _L0_ffn_ref(_layernorm(x, axis=-1)[None], L0_ffn_Wr, L0_ffn_br, L0_ffn_W1, L0_ffn_b1, L0_ffn_g1, L0_ffn_be1, L0_ffn_m1, L0_ffn_v1, L0_ffn_W2, L0_ffn_b2, L0_ffn_g2, L0_ffn_be2, L0_ffn_m2, L0_ffn_v2, L0_ffn_Wo, L0_ffn_bo)[0]
    return x

_drawn_inputs = setup_inputs


def setup_inputs(seed=0):
    import zlib

    import numpy as np

    out = dict(_drawn_inputs(seed))
    spreads = {'L0_ffn_br': (0.0, 0.318),
     'L0_ffn_b1': (0.0, 0.449),
     'L0_ffn_g1': (1.0, 0.2),
     'L0_ffn_be1': (0.0, 0.455),
     'L0_ffn_m1': (0.0, 0.442),
     'L0_ffn_v1': (1.0, 0.6),
     'L0_ffn_b2': (0.0, 0.32),
     'L0_ffn_g2': (1.0, 0.2),
     'L0_ffn_be2': (0.0, 0.336),
     'L0_ffn_m2': (0.0, 0.332),
     'L0_ffn_v2': (1.0, 0.6),
     'L0_ffn_bo': (0.0, 0.1)}
    factors = {'L0_mix_b_out': 4.111}
    for name, (base, spread) in spreads.items():
        noise = np.random.default_rng([zlib.crc32(name.encode()), seed]).standard_normal(out[name].shape)
        drawn = base * np.exp(spread * noise) if base else spread * noise
        out[name] = jnp.asarray(drawn.astype(out[name].dtype))
    for name, factor in factors.items():
        out[name] = (out[name] * factor).astype(out[name].dtype)
    return out
```

```python
from contextlib import ExitStack

import numpy as np

import concourse.bass as bass
from concourse import mybir

ALU = mybir.AluOpType
ACT = mybir.ActivationFunctionType
AX = mybir.AxisListType.X
F32 = mybir.dt.float32
BF16 = mybir.dt.bfloat16
I32 = mybir.dt.int32

P = 128
N, D = 6250, 256
HEADS, HD = 4, 64
NB = -(-N // P)
NPAD = NB * P
EDGES = 200000
CH = 4
GE = CH * P
NG = -(-EDGES // GE)
NX = NB - 1
SV = 8
NS = -(-(NG + NX) // SV)
NVT = 448
TT = NVT * CH // P
LROWS = NVT + 1
NODST = 7000
BIG = 1.0e34
HC = HD + 1
RW = HEADS * HC
TW = RW + HEADS
E, LN_EPS, BN_EPS, DIV_EPS, NORM_EPS = 8, 1e-5, 1e-3, 1e-7, 1e-12
IB = 7
NI = NB // IB
IN_ = IB * P
HN = IN_ // 2
SLOPE = 0.2
ONE = 1

C_ID, C_IOTA, C_VALID, C_GLAST, C_THR, C_W = 0, P, 2 * P, 2 * P + NB, 2 * P + NB + 1, 2 * P + NB + 2


def bc(ap, axis, n):
    a = ap.unsqueeze(axis)
    shape = list(a.shape)
    shape[axis] = n
    return a.to_broadcast(shape)


def chain(eng, sem):
    n = [0]

    def link(ins):
        n[0] += 1
        ins.then_inc(sem, 1)
        eng.wait_ge(sem, ONE + n[0])
    return link


def settle(eng, sem):
    eng.sem_inc(sem, 1)


class Mem:

    sems = []

    def __init__(self, nc, ctx):
        self.nc, self.ctx, self.counts = nc, ctx, []

    def sb(self, name, shape, dt=F32):
        return self.ctx.enter_context(self.nc.sbuf_tensor(name, shape, dt))

    def ps(self, name, shape, dt=F32):
        return self.ctx.enter_context(self.nc.psum_tensor(name, shape, dt))

    def sem(self, name):
        Mem.sems.append(self.nc.alloc_semaphore(name=name))
        return Mem.sems[-1]

    def count(self, name):
        self.counts.append(self.sem(name))
        return self.counts[-1]

    def start_counts(self, ahead=()):
        with self.nc.Block() as block:
            @block.gpsimd
            def _(pool):
                for c in self.counts:
                    pool.sem_inc(c, ONE)
                for c, n in ahead:
                    pool.sem_inc(c, n)

    @staticmethod
    def clear(nc):
        nc.clear_and_free_semaphores(Mem.sems)
        nc.all_engine_barrier()
        Mem.sems = []


def edge_lists(nc, io, dr, K):
    with ExitStack() as ctx:
        m = Mem(nc, ctx)
        first_i = m.sb("first_i", [1, NG], I32)
        row = m.sb("row", [1, NVT])
        blkf = m.sb("blkf", [1, NVT])
        base = m.sb("base", [1, NVT])
        brk = m.sb("brk_row", [1, NVT])
        pack = m.sb("pack", [1, NVT // 4])
        ones = m.sb("ones_l", [P, P])
        below = m.sb("below", [P, NG])
        cnt = m.sb("cnt", [P, 3])
        gidx = m.sb("gidx", [P, 1], I32)
        xrows = m.sb("xrows", [P, 2, GE], I32)
        base_bc = m.sb("base_bc", [P, NVT])
        raw = m.sb("raw", [P, 3, P], I32)
        rawf = m.sb("rawf", [P, 3, P])
        ps_row = m.ps("ps_row", [P, 512])
        ps_pen = m.ps("ps_pen", [P, 512])
        ps_base = m.ps("ps_base", [P, 512])
        ps_brk = m.ps("ps_brk", [P, 512])
        ps_t = [m.ps(f"ps_t{i}", [P, 512]) for i in range(3)]
        consts_in, first_in, copied, gathered, extra_in = map(m.sem, (
            "consts_in", "first_in", "lists_copied", "extra_gathered", "extra_stored"))
        firsts_f, first_bc, idx_ready, pen_t, rows_ready, rows_bc, base_ready = map(m.count, (
            "firsts_f", "first_bc", "idx_ready", "pen_t", "rows_ready", "rows_bc", "base_ready"))
        tile_in = m.sem("tile_in")
        dch, ones_set, cast, turned, spread = map(m.count, (
            "dve_chain_l", "ones_set_l", "tile_cast", "tile_turned", "tile_spread"))

        m.start_counts()
        with nc.Block() as block:
            @block.sync
            def _(sp):
                sp.dma_start(K.cst[:], io["cst"]).then_inc(consts_in, 16)
                sp.dma_start(row[:], io["cst_row"]).then_inc(consts_in, 16)
                sp.dma_start(first_i[:], io["firsts"]).then_inc(first_in, 16)
                for name in ("src", "dst"):
                    sp.dma_start(dr[name][0:NG, :], io[name][0:NG, :]).then_inc(copied, 16)
                    sp.dma_start(dr[name][NG + NX:LROWS, :], io[name][NG + NX:LROWS, :]).then_inc(copied, 16)
                sp.wait_ge(gathered, 32)
                for k, name in enumerate(("src", "dst")):
                    sp.dma_start(dr[name][NG:NG + NX, :], xrows[1:1 + NX, k, :]).then_inc(extra_in, 16)
                sp.wait_ge(copied, 64)
                sp.wait_ge(extra_in, 32)
                flat = {k: dr[k].rearrange("g e -> (g e)") for k in ("src", "dst")}
                with sp.Fori(0, TT) as t:
                    sp.wait_ge(spread, ONE + t * 3)
                    for k, (name, ahead) in enumerate((("dst", 0), ("dst", 1), ("src", 0))):
                        sp.dma_start(raw[:, k, :], flat[name][bass.ds(t * (P * P) + ahead, P * P)]
                                     .rearrange("(p e) -> p e", e=P)).then_inc(tile_in, 16)

            @block.gpsimd
            def _(pool):
                pool.wait_ge(idx_ready, ONE + 1)
                for k, name in enumerate(("src", "dst")):
                    pool.indirect_dma_start(xrows[:, k, :], None, io[name],
                                            bass.IndirectOffsetOnAxis(ap=gidx[:, 0:1], axis=0)).then_inc(gathered, 16)

            @block.tensor
            def _(pe):
                pe.wait_ge(ones_set, ONE + 1)
                pe.wait_ge(firsts_f, ONE + 1)
                pe.matmul(ps_row[:, 0:NG], ones[0:1, :], base[0:1, 0:NG], start=True, stop=True).then_inc(first_bc, 1)
                pe.wait_ge(idx_ready, ONE + 1)
                pe.transpose(ps_pen[0:1, 0:P], cnt[:, 2:3], K.cst[:, C_ID:C_ID + P]).then_inc(pen_t, 1)
                pe.wait_ge(rows_ready, ONE + 1)
                pe.matmul(ps_base[:, 0:NVT], ones[0:1, :], base[0:1, :], start=True, stop=True).then_inc(rows_bc, 1)
                pe.matmul(ps_brk[:, 0:NVT], ones[0:1, :], brk[0:1, :], start=True, stop=True).then_inc(rows_bc, 1)
                with pe.Fori(0, TT) as t:
                    pe.wait_ge(spread, ONE + t * 3)
                    pe.wait_ge(cast, ONE + t * 4 + 4)
                    for k in range(3):
                        pe.transpose(ps_t[k][:, 0:P], rawf[:, k, :], K.cst[:, C_ID:C_ID + P]).then_inc(turned, 1)

            @block.vector
            def _(dve):
                link = chain(dve, dch)
                dve.memset(ones[:], 1.0).then_inc(ones_set, 1)
                link(dve.memset(blkf[:], 0.0))
                dve.wait_ge(first_in, 16)
                dve.tensor_copy(base[0:1, 0:NG], first_i[:]).then_inc(firsts_f, 1)
                link(dve.tensor_scalar(first_i[:], first_i[:], 7, None, ALU.arith_shift_right))
                link(dve.tensor_copy(blkf[0:1, 0:NG], first_i[:]))
                dve.wait_ge(consts_in, 32)
                link(dve.tensor_copy(blkf[0:1, NG:NG + NX], row[0:1, NG:NG + NX]))
                link(dve.tensor_copy(K.cstb[:], K.cst[:, 0:2 * P]))
                dve.wait_ge(first_bc, ONE + 1)
                link(dve.tensor_scalar(below[:], ps_row[:, 0:NG], K.cst[:, C_THR:C_THR + 1], None, ALU.is_lt))
                link(dve.tensor_reduce(cnt[:, 0:1], below[:], AX, ALU.add))
                link(dve.tensor_scalar(cnt[:, 1:2], cnt[:, 0:1], -1.0, 0.0, ALU.add, ALU.max))
                link(dve.tensor_scalar(cnt[:, 2:3], cnt[:, 0:1], 0.0, -1.0e6, ALU.is_equal, ALU.mult))
                dve.tensor_copy(gidx[:], cnt[:, 1:2]).then_inc(idx_ready, 1)
                dve.wait_ge(pen_t, ONE + 1)
                link(dve.tensor_scalar(base[:], blkf[:], float(P), None, ALU.mult))
                link(dve.tensor_tensor(base[0:1, NG:NG + NX], base[0:1, NG:NG + NX], ps_pen[0:1, 1:1 + NX], ALU.add))
                link(dve.memset(brk[:], 0.0))
                link(dve.tensor_tensor(brk[0:1, 1:NVT], blkf[0:1, 1:NVT], blkf[0:1, 0:NVT - 1], ALU.is_equal))
                link(dve.memset(brk[0:1, 0:NVT:SV], 0.0))
                link(dve.tensor_scalar(brk[:], brk[:], -1.0, BIG, ALU.add, ALU.mult))
                dve.engine_nop().then_inc(rows_ready, 1)
                b4 = blkf[:].rearrange("p (a b) -> p a b", b=4)
                pk = pack[:].unsqueeze(2)
                link(dve.scalar_tensor_tensor(pk, b4[:, :, 3:4], 64.0, b4[:, :, 2:3], ALU.mult, ALU.add))
                link(dve.scalar_tensor_tensor(pk, pk, 64.0, b4[:, :, 1:2], ALU.mult, ALU.add))
                link(dve.scalar_tensor_tensor(K.blk[:].unsqueeze(2), pk, 64.0, b4[:, :, 0:1], ALU.mult, ALU.add))
                dve.wait_ge(rows_bc, ONE + 2)
                dve.tensor_copy(base_bc[:], ps_base[:, 0:NVT]).then_inc(base_ready, 1)
                dve.tensor_copy(K.brk[:], bc(ps_brk[:, 0:NVT].rearrange("p (s v) -> p s v", v=SV), 2, HEADS))\
                   .then_inc(base_ready, 1)
                dve.wait_ge(base_ready, ONE + 2)
                with dve.Fori(0, TT) as t:
                    dve.wait_ge(tile_in, t * 48 + 48)
                    dve.wait_ge(turned, ONE + t * 3)
                    dve.tensor_copy(rawf[:, 0, :], raw[:, 0, :]).then_inc(cast, 1)
                    dve.tensor_copy(rawf[:, 1, :], raw[:, 2, :]).then_inc(cast, 1)
                    dve.tensor_tensor(rawf[:, 2, :], raw[:, 0, :], raw[:, 1, :], ALU.not_equal).then_inc(cast, 1)
                    dve.wait_ge(cast, ONE + t * 4 + 3)
                    dve.tensor_tensor(rawf[:, 2, P - 1:P], rawf[:, 2, P - 1:P], K.cst[:, C_GLAST:C_GLAST + 1],
                                      ALU.max).then_inc(cast, 1)
                    dve.wait_ge(turned, ONE + t * 3 + 3)
                    at = bass.ds(t * P, P)
                    dve.tensor_tensor(K.rel[:, at].rearrange("p (v j) -> p v j", j=CH),
                                      ps_t[0][:, 0:P].rearrange("p (v j) -> p v j", j=CH),
                                      bc(base_bc[:, bass.ds(t * (P // CH), P // CH)], 2, CH),
                                      ALU.subtract).then_inc(spread, 1)
                    dve.tensor_copy(K.ix[:, at], ps_t[1][:, 0:P]).then_inc(spread, 1)
                    dve.tensor_copy(K.last[:, at], ps_t[2][:, 0:P]).then_inc(spread, 1)


def weights(nc, io, K):
    with ExitStack() as ctx:
        m = Mem(nc, ctx)
        wqkv = m.sb("wqkv", [P, 2, 3 * D])
        bqkv = m.sb("bqkv", [P, 3 * D])
        wout = m.sb("wout", [P, 2, D])
        bout = m.sb("bout", [P, D])
        bvc = m.sb("bvc", [P, 2])
        bvr = m.sb("bvr", [P, 2, P])
        att = m.sb("att", [P, 2, D])
        prod = m.sb("prod", [P, 2, D])
        mean = m.sb("mean_w", [P, 6])
        bnp = m.sb("bnp", [P, 10, 2 * E])
        std = m.sb("bn_std", [P, 2, 2 * E])
        wvt = m.sb("wvt", [P, 2, 2, P])
        ps = [m.ps(f"ps_w{i}", [P, 512]) for i in range(4)]
        w_in = m.sem("w_in")
        dch, turned, wvt_ready, wvo, bvw, bvr_ready, var_ready, std_ready = map(m.count, (
            "dve_chain_w", "wv_turned", "wvt_ready", "wvo_done", "bvw_done", "bvr_ready", "bn_var", "bn_std"))
        m.start_counts()
        with nc.Block() as block:
            @block.sync
            def _(sp):
                for dst, src in ((wqkv[:], io["w_qkv"]), (wout[:], io["w_out"]), (bvc[:], io["bv_col"]),
                                 (bqkv[:], io["b_qkv"].partition_broadcast(P)),
                                 (bout[:], io["b_out"].partition_broadcast(P)),
                                 (att[:, 0, :], io["att_src"].partition_broadcast(P)),
                                 (att[:, 1, :], io["att_dst"].partition_broadcast(P)),
                                 (K.wcat[:, :, 0:D], io["w_gat"]), (bnp[:], io["bn"]),
                                 (K.wr[:], io["w_r"]), (K.br[:], io["b_r"].partition_broadcast(P)),
                                 (K.bo[0:E, :], io["b_o"])):
                    sp.dma_start(dst, src).then_inc(w_in, 16)

            @block.scalar
            def _(act):
                act.wait_ge(var_ready, ONE + 1)
                act.activation(std[:], bnp[:, 8:10, :], ACT.Sqrt).then_inc(std_ready, 1)

            @block.tensor
            def _(pe):
                pe.wait_ge(w_in, 12 * 16)
                for ch in range(2):
                    for kh in range(2):
                        pe.transpose(ps[ch][:, kh * P:(kh + 1) * P],
                                     wqkv[:, kh, 2 * D + ch * P:2 * D + (ch + 1) * P],
                                     K.cst[:, C_ID:C_ID + P]).then_inc(turned, 1)
                pe.wait_ge(wvt_ready, ONE + 2)
                for mh in range(2):
                    for ch in range(2):
                        pe.matmul(ps[2][:, mh * D:(mh + 1) * D], wvt[:, ch, mh, :], wout[:, ch, :],
                                  start=(ch == 0), stop=(ch == 1)).then_inc(wvo, 1)
                pe.wait_ge(bvr_ready, ONE + 1)
                for ch in range(2):
                    pe.matmul(ps[3][:, 0:D], bvr[:, ch, :], wout[:, ch, :],
                              start=(ch == 0), stop=(ch == 1)).then_inc(bvw, 1)

            @block.vector
            def _(dve):
                link = chain(dve, dch)
                dve.wait_ge(w_in, 12 * 16)
                for kh in range(2):
                    for a in range(2):
                        link(dve.tensor_tensor(prod[:, a, :], K.wcat[:, kh, 0:D], att[:, a, :], ALU.mult))
                    for a in range(2):
                        link(dve.tensor_reduce(K.wcat[:, kh, D + 4 * a:D + 4 * a + 4],
                                               prod[:, a, :].rearrange("p (h c) -> p h c", c=HD), AX, ALU.add))
                for i in range(2):
                    link(dve.tensor_reduce(mean[:, 3 * i:3 * i + 2], wqkv[:, :, i * D:(i + 1) * D], AX, ALU.add))
                    link(dve.tensor_reduce(mean[:, 3 * i + 2:3 * i + 3], bqkv[:, i * D:(i + 1) * D], AX, ALU.add))
                link(dve.tensor_scalar(mean[:], mean[:], 1.0 / D, None, ALU.mult))
                for i, (w, b) in enumerate(((K.wq, K.bq), (K.wk, K.bk))):
                    for kh in range(2):
                        link(dve.tensor_scalar(w[:, kh, :], wqkv[:, kh, i * D:(i + 1) * D],
                                               mean[:, 3 * i + kh:3 * i + kh + 1], None, ALU.subtract))
                    link(dve.tensor_scalar(b[:], bqkv[:, i * D:(i + 1) * D],
                                           mean[:, 3 * i + 2:3 * i + 3], None, ALU.subtract))
                dve.tensor_copy(bvr[:], bc(bvc[:], 2, P)).then_inc(bvr_ready, 1)
                link(dve.tensor_scalar(bnp[:, 8:10, :], bnp[:, 8:10, :], BN_EPS, None, ALU.add))
                dve.engine_nop().then_inc(var_ready, 1)
                dve.wait_ge(std_ready, ONE + 1)
                link(dve.reciprocal(std[:], std[:]))
                link(dve.tensor_tensor(K.bns[:], bnp[:, 2:4, :], std[:], ALU.mult))
                link(dve.tensor_tensor(bnp[:, 0:2, :], bnp[:, 0:2, :], bnp[:, 6:8, :], ALU.subtract))
                link(dve.tensor_tensor(bnp[:, 0:2, :], bnp[:, 0:2, :], K.bns[:], ALU.mult))
                link(dve.tensor_tensor(K.bnb[:], bnp[:, 0:2, :], bnp[:, 4:6, :], ALU.add))
                dve.wait_ge(turned, ONE + 4)
                for ch in range(2):
                    dve.tensor_copy(wvt[:, ch, :, :], ps[ch][:, 0:D].rearrange("p (a b) -> p a b", b=P)).then_inc(wvt_ready, 1)
                dve.wait_ge(wvo, ONE + 4)
                link(dve.tensor_copy(K.wvo[:], ps[2][:].rearrange("p (a b) -> p a b", b=D)))
                dve.wait_ge(bvw, ONE + 2)
                link(dve.tensor_copy(K.bvw[:], ps[3][:, 0:D]))
                link(dve.tensor_tensor(K.cb[:], K.bvw[:], bout[:], ALU.add))


def project(nc, io, dr, K):
    with ExitStack() as ctx:
        m = Mem(nc, ctx)
        x7 = m.sb("x7", [P, IB, D])
        xn7 = m.sb("xn7", [P, IB, D])
        xnt7 = m.sb("xnt7", [P, IB, 2, P])
        rows7 = m.sb("rows7", [P, IB, RW + 2 * HEADS])
        k7 = m.sb("k7", [P, IB, D])
        ks7 = m.sb("ks7", [P, 3, IB])
        kk7 = m.sb("kk7", [P, IB, D])
        stats = m.sb("stats", [P, IB, 6])
        mv = m.sb("mv", [P, IB, 2])
        var = m.sb("var", [P, 2, IB])
        ones = m.sb("ones_p", [P, 2])
        zeros = m.sb("zeros_p", [P, 512])
        att = m.sb("at_sb", [P, 2, D])
        ssb = m.sb("s_sb", [P, 8])
        ps_t = [m.ps(f"ps_xt{i}", [P, 512]) for i in range(2)]
        ps_p = [m.ps(f"ps_p{i}", [P, 512]) for i in range(2)]
        ps_k = [m.ps(f"ps_k{i}", [P, 512]) for i in range(2)]
        ps_a = m.ps("ps_a", [P, 512])
        ps_s = m.ps("ps_s", [P, 512])
        settled, stored = m.count("settled_p"), m.count("stored_p")
        x_in, xnt_stored, rows_stored = m.sem("x_in"), m.sem("xnt_stored"), m.sem("rows_stored")
        (set_, stats_d, aggr_d, var_d, std_d, rstd_d, xn_d, turned, xnt_d, proj_d, k_d, rows_d, kb_d, k2_d,
         r1_d, r2_d, r3_d, kn_d, kk_d, sums_d, init_d, fin, dch, end_sq, end_mm) = map(m.count, (
            "consts_set_p", "stats_done", "aggr_done", "var_done", "std_done", "rstd_done", "xn_done", "x_turned",
            "xnt_done", "proj_done", "k_done", "rows_done", "k_biased", "k_squared", "r1_done", "r2_done", "r3_done",
            "k_normed", "k_fourth", "sums_done", "state_set", "all_summed", "dve_chain_p", "end_sqrt", "end_mm"))
        m.start_counts()
        with nc.Block() as block:
            @block.sync
            def _(sp):
                with sp.Fori(0, NI) as i:
                    sp.wait_ge(xn_d, ONE + i * IB)
                    sp.dma_start(x7[:], io["x"][bass.ds(i * IN_, IN_), :].rearrange("(j p) c -> p j c", p=P)).then_inc(x_in, 16)

            @block.gpsimd
            def _(pool):
                with pool.Fori(0, NI) as i:
                    pool.wait_ge(xnt_d, ONE + i * IB + IB)
                    pool.dma_start(dr["xnt"][bass.ds(i, 1)].rearrange("o p c -> (o p) c"),
                                   xnt7[:].rearrange("p j k n -> p (j k n)")).then_inc(xnt_stored, 16)
                    pool.wait_ge(rows_d, ONE + i * IB + IB)
                    pool.dma_start(dr["table"][bass.ds(i * IN_, IN_), :].rearrange("(j p) c -> p j c", p=P),
                                   rows7[:, :, 0:TW]).then_inc(rows_stored, 16)
                    pool.wait_ge(xnt_stored, i * 16 + 16)
                    pool.wait_ge(rows_stored, i * 16 + 16)
                    pool.sem_inc(stored, 1)

            @block.tensor
            def _(pe):
                pe.wait_ge(set_, ONE + 3)
                pe.matmul(ps_a[:, :], zeros[:, 0:P], zeros[:, :], start=True, stop=False, skip_group_check=True)
                pe.matmul(ps_s[:, 0:8], zeros[:, 0:P], zeros[:, 0:8], start=True, stop=False, skip_group_check=True)
                with pe.Fori(0, NI) as i:
                    for j in range(IB):
                        pe.wait_ge(xn_d, ONE + i * IB + (j + 1))
                        pe.wait_ge(xnt_d, ONE + i * IB + max(j - 1, 0))
                        for kh in range(2):
                            pe.transpose(ps_t[j % 2][:, kh * P:(kh + 1) * P], xn7[:, j, kh * P:(kh + 1) * P],
                                         K.cst[:, C_ID:C_ID + P]).then_inc(turned, 1)
                    for j in range(IB):
                        pe.wait_ge(xnt_d, ONE + i * IB + (j + 1))
                        pe.wait_ge(rows_d, ONE + i * IB + max(j - 1, 0))
                        for kh in range(2):
                            mm = pe.matmul(ps_p[j % 2][:, 0:D + 2 * HEADS], xnt7[:, j, kh, :], K.wcat[:, kh, :],
                                           start=(kh == 0), stop=(kh == 1))
                        mm.then_inc(proj_d, 1)
                        pe.wait_ge(kb_d, ONE + i * IB + max(j - 1, 0))
                        for kh in range(2):
                            mm = pe.matmul(ps_k[j % 2][:, 0:D], xnt7[:, j, kh, :], K.wk[:, kh, :],
                                           start=(kh == 0), stop=(kh == 1))
                        mm.then_inc(k_d, 1)
                    for j in range(IB):
                        pe.wait_ge(kn_d, ONE + i * IB + (j + 1))
                        for kh in range(2):
                            pe.matmul(ps_a[:, kh * D:(kh + 1) * D], xn7[:, j, kh * P:(kh + 1) * P], k7[:, j, :],
                                      start=False, stop=False, skip_group_check=True)
                        for kh in range(2):
                            pe.matmul(ps_s[:, kh:kh + 1], k7[:, j, kh * P:(kh + 1) * P], ones[:, 0:1],
                                      start=False, stop=False, skip_group_check=True)
                        pe.wait_ge(kk_d, ONE + i * IB + (j + 1))
                        for kh in range(2):
                            mm = pe.matmul(ps_s[:, 2 + kh:3 + kh], kk7[:, j, kh * P:(kh + 1) * P], ones[:, 0:1],
                                           start=False, stop=False, skip_group_check=True)
                        mm.then_inc(sums_d, 1)
                pe.wait_ge(fin, ONE + 2)
                for mh in range(2):
                    for kh in range(2):
                        pe.matmul(ps_p[mh][:, 0:D], att[:, kh, mh * P:(mh + 1) * P], K.wvo[:, kh, :],
                                  start=(kh == 0), stop=(kh == 1)).then_inc(end_mm, 1)

            @block.scalar
            def _(act):
                with act.Fori(0, NI) as i:
                    act.wait_ge(var_d, ONE + i + 1)
                    act.activation(var[:, 1, :], var[:, 0, :], ACT.Sqrt).then_inc(std_d, 1)
                    for j in range(IB):
                        if j == 0:
                            act.wait_ge(stored, ONE + i * 1)
                            act.wait_ge(init_d, ONE + i * 2)
                        act.wait_ge(proj_d, ONE + i * IB + (j + 1))
                        act.copy(rows7[:, j, 0:RW].rearrange("p (h c) -> p h c", c=HC)[:, :, 0:HD],
                                 ps_p[j % 2][:, 0:D].rearrange("p (h c) -> p h c", c=HD))
                        act.copy(rows7[:, j, RW:RW + 2 * HEADS], ps_p[j % 2][:, D:D + 2 * HEADS]).then_inc(rows_d, 1)
                        act.wait_ge(kb_d, ONE + i * IB + (j + 1))
                        act.activation(k7[:, j, :], k7[:, j, :], ACT.Square, accum_out=ks7[:, 0, j:j + 1]).then_inc(k2_d, 1)
                    act.wait_ge(sums_d, ONE + i * IB)
                    for j in range(IB):
                        act.wait_ge(kn_d, ONE + i * IB + (j + 1))
                        act.activation(kk7[:, j, :], k7[:, j, :], ACT.Square).then_inc(kk_d, 1)
                act.wait_ge(fin, ONE + 2)
                act.activation(ssb[:, 4:6], ssb[:, 2:4], ACT.Sqrt).then_inc(end_sq, 1)

            @block.vector
            def _(dve):
                dve.memset(ones[:], 1.0).then_inc(set_, 1)
                dve.memset(zeros[:], 0.0).then_inc(set_, 1)
                dve.memset(rows7[:], 1.0).then_inc(set_, 1)
                with dve.Fori(0, NI) as i:
                    dve.wait_ge(x_in, i * 16 + 16)
                    for j in range(IB):
                        dve.bn_stats(stats[:, j, :], x7[:, j, :]).then_inc(stats_d, 1)
                    for j in range(IB):
                        if j == 0:
                            dve.wait_ge(stats_d, ONE + i * IB + IB)
                            settle(dve, settled)
                        dve.bn_aggr(mv[:, j, :], stats[:, j, :]).then_inc(aggr_d, 1)
                    dve.wait_ge(aggr_d, ONE + i * IB + IB)
                    dve.tensor_scalar(var[:, 0, :].unsqueeze(2), mv[:, :, 1:2], LN_EPS, None, ALU.add).then_inc(var_d, 1)
                    dve.wait_ge(std_d, ONE + i + 1)
                    dve.reciprocal(var[:, 1, :], var[:, 1, :]).then_inc(rstd_d, 1)
                    dve.wait_ge(rstd_d, ONE + i + 1)
                    dve.wait_ge(sums_d, ONE + i * IB)
                    for j in range(IB):
                        dve.tensor_scalar(xn7[:, j, :], x7[:, j, :], mv[:, j, 0:1], var[:, 1, j:j + 1],
                                          ALU.subtract, ALU.mult).then_inc(xn_d, 1)
                    dve.wait_ge(stored, ONE + i * 1)
                    dve.wait_ge(k_d, ONE + i * IB)
                    for j in range(IB):
                        dve.wait_ge(turned, ONE + i * (2 * IB) + 2 * (j + 1))
                        dve.tensor_copy(xnt7[:, j, :, :].rearrange("p k n -> p (k n)"), ps_t[j % 2][:, 0:2 * P]).then_inc(xnt_d, 1)
                    for j in range(IB):
                        dve.wait_ge(k_d, ONE + i * IB + (j + 1))
                        dve.tensor_tensor(k7[:, j, :], ps_k[j % 2][:, 0:D], K.bk[:], ALU.add).then_inc(kb_d, 1)
                    dve.wait_ge(rows_d, ONE + i * IB + IB)
                    settle(dve, settled)
                    at = bass.ds(i * IB, IB)
                    dve.tensor_copy(K.acc[:, at, :], rows7[:, :, 0:RW]).then_inc(init_d, 1)
                    dve.tensor_copy(K.state[:, at, :], rows7[:, :, RW:RW + 2 * HEADS]).then_inc(init_d, 1)
                    dve.wait_ge(k2_d, ONE + i * IB + IB)
                    dve.tensor_scalar(ks7[:, 1, :], ks7[:, 0, :], DIV_EPS, None, ALU.add).then_inc(r1_d, 1)
                    dve.wait_ge(r1_d, ONE + i + 1)
                    dve.reciprocal(ks7[:, 2, :], ks7[:, 1, :]).then_inc(r2_d, 1)
                    dve.wait_ge(r2_d, ONE + i + 1)
                    dve.tensor_tensor(ks7[:, 1, :], ks7[:, 2, :], K.cst[:, bass.ds(i * IB + C_VALID, IB)], ALU.mult).then_inc(r3_d, 1)
                    dve.wait_ge(r3_d, ONE + i + 1)
                    for j in range(IB):
                        dve.tensor_scalar(k7[:, j, :], k7[:, j, :], ks7[:, 1, j:j + 1], None, ALU.mult).then_inc(kn_d, 1)
                link = chain(dve, dch)
                dve.wait_ge(sums_d, ONE + NI * IB)
                dve.tensor_copy(att[:], ps_a[:].rearrange("p (a b) -> p a b", b=D)).then_inc(fin, 1)
                dve.tensor_copy(ssb[:, 0:4], ps_s[:, 0:4]).then_inc(fin, 1)
                dve.wait_ge(end_sq, ONE + 1)
                link(dve.tensor_scalar(ssb[:, 6:8], ssb[:, 4:6], NORM_EPS, float(N) ** 0.5, ALU.max, ALU.mult))
                link(dve.reciprocal(ssb[:, 6:8], ssb[:, 6:8]))
                dve.wait_ge(end_mm, ONE + 4)
                for mh in range(2):
                    link(dve.scalar_tensor_tensor(K.kvw[:, mh, :], K.bvw[:], ssb[:, mh:mh + 1], ps_p[mh][:, 0:D],
                                                  ALU.mult, ALU.add))
                    link(dve.tensor_scalar(K.kvw[:, mh, :], K.kvw[:, mh, :], ssb[:, 6 + mh:7 + mh], None, ALU.mult))


def attend(nc, dr, K):
    with ExitStack() as ctx:
        m = Mem(nc, ctx)
        xg = [m.sb(f"xg{q}", [P, SV, CH, TW]) for q in range(2)]
        idx = [m.sb(f"idx{q}", [P, SV * CH], I32) for q in range(2)]
        hot = [m.sb(f"hot{q}", [P, SV, CH, P], BF16) for q in range(2)]
        hotw = [m.sb(f"hotw{q}", [P, CH, P]) for q in range(2)]
        hot_t = m.sb("hot_t", [P, SV, CH * P], BF16)
        y = [m.sb(f"y{q}", [P, CH, RW]) for q in range(2)]
        dlist = [m.sb(f"dlist{q}", [HEADS * SV, GE], I32) for q in range(2)]
        dbig = m.sb("dbig", [HEADS * SV, GE])
        step_ = m.sb("seg_step", [HEADS * SV, GE])
        asrc = m.sb("asrc", [P, CH, HEADS, SV])
        fmax = m.sb("fmax", [HEADS * SV, GE])
        tails = m.sb("tails", [P, 2, SV, CH, HEADS])
        tail = m.sb("tail", [P, SV, CH, 3 * HEADS + 1], BF16)
        pair_rest = m.sb("pair_rest", [P, 2, HEADS * SV])
        pair = m.sb("pair", [P, 3, 2 * HEADS, SV], BF16)
        st = m.sb("st", [P, 4 + 3 * HEADS * SV])
        sv_ = m.sb("sv", [P, HEADS * SV])
        gone = m.sb("gone", [P, SV])
        zz = m.sb("zz", [P, 4, HEADS * SV])
        fo = m.sb("fo", [P, HEADS * SV])
        sc = m.sb("sc", [P, SV * CH * HEADS])
        w = m.sb("w", [P, SV * CH, HEADS])
        ps_t, ps_f, ps_m, ps_l = (m.ps(n, [P, 512]) for n in ("ps_at", "ps_f", "ps_m", "ps_l"))
        ps_o = [m.ps(f"ps_o{i}", [P, 2 * CH * P], BF16) for i in range(2)]
        ps_y = [m.ps(f"ps_y{i}", [P, 512]) for i in range(2)]
        got = [[m.sem(f"gathered{q}_{v}") for v in range(SV)] for q in range(2)]
        settled = m.count("settled_a")
        dl_in = [m.sem(f"dlist_in{q}") for q in range(2)]
        (idx_d, hot_d, dbig_d, step_d, at_d, fmax_d, ft_d, tail_d, sm_d, loaded, gone_d, sv_d, mx_d, run_d,
         saved, old1, old_d, z_d, lk_d, fa_d, fo_d, ho_d, ht_d, look_d, s1_d, s2_d, s3_d, s4_d, w_d,
         hotw_d, ya_d, msum_d, tp1_d, tp2_d, tp3_d, pp_d, z1_d, lk1_d,
         y_d, py_d, sc_d, acc_d, pool_i, as_d) = map(m.count, (
            "idx_staged", "hot_built", "dst_scaled", "segments_done", "asrc_turned", "fmax_done", "fmax_turned",
            "tails_done", "max_summed", "state_loaded", "gone_done", "sv_done", "max_with_state", "running_max",
            "state_saved", "old_shifted", "old_done", "fold_z", "fold_leaky", "fold_arg", "fold_done", "hot_turned",
            "hot_t_done", "looked_up", "score_z", "score_leaky", "score_less", "score_capped",
            "weights_done", "hot_widened", "y_done_act", "max_joined", "tail_first", "tail_second", "tail_third",
            "pair_parts", "max_shifted", "max_leaky", "y_done", "y_summed", "acc_scaled", "acc_done", "idx_free", "asrc_packed"))
        NM = 3 * HEADS + 1
        YV = CH - 1
        SN, S0, S1, S2 = 1, 1, 1 + HEADS * SV, 1 + 2 * HEADS * SV

        def hv(t, at):
            return t[:, at:at + HEADS * SV].rearrange("p (h v) -> p h v", v=SV)

        def steps(eng, body):
            with eng.Fori(0, NS // 2) as i:
                for q in range(2):
                    body(q, i, lambda k, q=q, i=i: i * (2 * k) + q * k)
            if NS % 2:
                body(0, NS // 2, lambda k: (NS - 1) * k)

        m.start_counts(((y_d, 2 * SV), (ya_d, 2 * SV), (dbig_d, 1), (as_d, 1)))
        with nc.Block() as block:
            @block.gpsimd
            def _(pool):
                for q in range(2):
                    pool.memset(idx[q][:], 0).then_inc(pool_i, 1)
                pool.wait_ge(pool_i, ONE + 2)

                def body(q, i, n):
                    pool.wait_ge(as_d, ONE + n(1))
                    pool.tensor_copy(idx[q][:], K.ix[:, bass.ds(n(SV * CH), SV * CH)]).then_inc(idx_d, 1)
                    pool.wait_ge(idx_d, ONE + n(1) + 1)
                    for v in range(SV):
                        pool.wait_ge(y_d, ONE + n(SV) + (v + 1))
                        pool.wait_ge(ya_d, ONE + n(SV) + (v + 1))
                        settle(pool, settled)
                        for j in range(CH):
                            c = v * CH + j
                            pool.indirect_dma_start(
                                xg[q][:, v, j, :], None, dr["table"],
                                bass.IndirectOffsetOnAxis(ap=idx[q][:, c:c + 1], axis=0)).then_inc(got[q][v], 16)
                steps(pool, body)

            @block.sync
            def _(sp):
                def body(q, i, n):
                    sp.wait_ge(dbig_d, ONE + n(1))
                    for h in range(HEADS):
                        sp.dma_start(dlist[q][h * SV:(h + 1) * SV, :],
                                     dr["dst"][bass.ds(n(SV), SV), :]).then_inc(dl_in[q], 16)
                steps(sp, body)

            @block.scalar
            def _(act):
                def body(q, i, n):
                    act.wait_ge(dl_in[q], i * (16 * HEADS) + 16 * HEADS)
                    act.wait_ge(step_d, ONE + n(2))
                    act.mul(dbig[:], dlist[q][:], BIG).then_inc(dbig_d, 1)
                    for v in range(SV):
                        act.wait_ge(got[q][v], i * (16 * CH) + 16 * CH)
                    act.wait_ge(at_d, ONE + n(CH))
                    act.copy(asrc[:], xg[q][:, :, :, RW:TW].rearrange("p v j h -> p j h v")).then_inc(as_d, 1)
                    act.wait_ge(look_d, ONE + n(1))
                    for p in range(SV // 2):
                        act.wait_ge(ho_d, ONE + n(SV // 2) + (p + 1))
                        act.copy(hot_t[:, 2 * p:2 * p + 2, :].rearrange("p v n -> p (v n)"), ps_o[p % 2][:]).then_inc(ht_d, 1)
                    for v in range(2):
                        widen(v, q, n)
                    act.wait_ge(fa_d, ONE + n(1) + 1)
                    act.wait_ge(acc_d, ONE + n(SV))
                    act.activation(fo[:], zz[:, 3, :], ACT.Exp).then_inc(fo_d, 1)
                    act.wait_ge(s4_d, ONE + n(1) + 1)
                    act.activation(w[:], sc[:].rearrange("p (c h) -> p c h", h=HEADS), ACT.Exp).then_inc(w_d, 1)
                    for v in range(SV):
                        if v >= 2:
                            widen(v, q, n)
                        act.wait_ge(w_d, ONE + n(1) + 1)
                        act.wait_ge(py_d, ONE + n(SV) + max(v - 1, 0))
                        for h in range(HEADS):
                            at = slice(h * HC, (h + 1) * HC)
                            mul = act.activation(y[v % 2][:, YV, at], xg[q][:, v, YV, at], ACT.Copy,
                                                 scale=w[:, v * CH + YV, h:h + 1])
                        mul.then_inc(ya_d, 1)

                def widen(v, q, n):
                    act.wait_ge(hot_d, ONE + n(4) + 4)
                    act.wait_ge(py_d, ONE + n(SV) + max(v - 1, 0))
                    act.copy(hotw[v % 2][:], hot[q][:, v, :, :]).then_inc(hotw_d, 1)
                steps(act, body)

            @block.tensor
            def _(pe):
                ident = K.cst[:, C_ID:C_ID + P]

                def body(q, i, n):
                    pe.wait_ge(fmax_d, ONE + n(1))
                    pe.wait_ge(as_d, ONE + n(1) + 2)
                    for j in range(CH):
                        pe.transpose(ps_t[0:HEADS * SV, j * P:(j + 1) * P],
                                     asrc[:, j, :, :].rearrange("p h v -> p (h v)"), ident).then_inc(at_d, 1)
                    pe.wait_ge(hot_d, ONE + n(4) + 4)
                    for v in range(SV):
                        p = v // 2
                        pe.wait_ge(ht_d, ONE + n(SV // 2) + max(p - 1, 0))
                        for j in range(CH):
                            at = (v % 2 * CH + j) * P
                            mm = pe.transpose(ps_o[p % 2][:, at:at + P], hot[q][:, v, j, :], K.cstb[:, 0:P])
                        if v % 2:
                            mm.then_inc(ho_d, 1)
                    pe.wait_ge(fmax_d, ONE + n(1) + 1)
                    pe.wait_ge(tail_d, ONE + n(2))
                    settle(pe, settled)
                    for j in range(CH):
                        pe.transpose(ps_f[:, j * HEADS * SV:(j + 1) * HEADS * SV], fmax[:, j * P:(j + 1) * P],
                                     ident[0:HEADS * SV, 0:HEADS * SV]).then_inc(ft_d, 1)
                    pe.wait_ge(tp3_d, ONE + n(1) + 1)
                    pe.wait_ge(sv_d, ONE + n(1))
                    for v in range(SV):
                        for j in range(CH):
                            mm = pe.matmul(ps_m[:, v * NM:(v + 1) * NM], hot[q][:, v, j, :], tail[:, v, j, :],
                                           start=(j == 0), stop=(j == CH - 1))
                    mm.then_inc(sm_d, 1)
                    pe.wait_ge(ht_d, ONE + n(SV // 2) + SV // 2)
                    pe.wait_ge(pp_d, ONE + n(8) + 8)
                    pe.wait_ge(s3_d, ONE + n(1))
                    for v in range(SV):
                        for j in range(CH):
                            c = v * CH + j
                            for k in range(3):
                                mm = pe.matmul(ps_l[:, c * 8:c * 8 + 8], hot_t[:, v, j * P:(j + 1) * P], pair[:, k, :, v],
                                               start=(k == 0), stop=(k == 2))
                    mm.then_inc(look_d, 1)
                    for v in range(SV):
                        pe.wait_ge(hotw_d, ONE + n(SV) + (v + 1))
                        pe.wait_ge(y_d, ONE + n(SV) + (2 * SV + v + 1))
                        pe.wait_ge(acc_d, ONE + n(SV) + max(v - 1, 0))
                        for j in range(CH):
                            if j == YV:
                                pe.wait_ge(ya_d, ONE + n(SV) + (2 * SV + v + 1))
                            mm = pe.matmul(ps_y[v % 2][:, 0:RW], hotw[v % 2][:, j, :], y[v % 2][:, j, :],
                                           start=(j == 0), stop=(j == CH - 1))
                        mm.then_inc(py_d, 1)
                steps(pe, body)

            @block.vector
            def _(dve):
                dve.memset(st[:], 0.0).then_inc(gone_d, 1)
                dve.wait_ge(gone_d, ONE + 1)
                flat = HEADS * SV

                def build(part, q, at):
                    k = SV // 4
                    rel = K.rel[:, bass.ds(at + part * (k * CH), k * CH)]
                    dve.tensor_tensor(hot[q][:, part * k:(part + 1) * k, :, :].rearrange("p v j n -> p (v j) n"),
                                      bc(K.cstb[:, P:2 * P], 1, k * CH), bc(rel, 2, P), ALU.is_equal).then_inc(hot_d, 1)
                for part in range(4):
                    build(part, 0, 0)

                def body(q, i, n):
                    nxt = 1 - q, n(SV * CH) + SV * CH
                    dve.wait_ge(hotw_d, ONE + n(SV))
                    build(0, *nxt)
                    words = [dve.value_load(K.blk[0:1, bass.ds(n(2) + k, 1)], min_val=0, max_val=(1 << 24) - 1)
                             for k in range(2)]
                    blk = [nc.s_assert_within(dve.snap((words[v // 4] >> (6 * (v % 4))) & 63), 0, NB - 1, skip_runtime_bounds_check_because="destinations are nodes")
                           for v in range(SV)]
                    dve.wait_ge(dbig_d, ONE + n(1) + 2)
                    dve.memset(step_[:, 0:1], 0.0).then_inc(step_d, 1)
                    dve.tensor_tensor(step_[:, 1:GE], dbig[:, 0:GE - 1], dbig[:, 1:GE], ALU.subtract).then_inc(step_d, 1)
                    dve.wait_ge(step_d, ONE + n(2) + 2)
                    dve.wait_ge(at_d, ONE + n(CH) + CH)
                    dve.tensor_tensor_scan(fmax[:], step_[:], ps_t[0:flat, :], -BIG, ALU.add, ALU.max).then_inc(fmax_d, 1)
                    last = K.last[:, bass.ds(n(SV * CH), SV * CH)].rearrange("p (v j) -> p v j", j=CH)
                    dve.wait_ge(ft_d, ONE + n(CH) + CH)
                    dve.wait_ge(sm_d, ONE + n(1))
                    kept = ps_f[:, 0:CH * flat].rearrange("p (j h v) -> p h v j", h=HEADS, v=SV)
                    parts = [tail[:, :, :, k * HEADS:(k + 1) * HEADS] for k in range(3)]
                    dve.tensor_tensor(parts[0].rearrange("p v j h -> p h v j"), kept, bc(last, 1, HEADS), ALU.mult).then_inc(tp1_d, 1)
                    dve.tensor_tensor(tails[:, 0].rearrange("p v j h -> p h v j"), kept, bc(last, 1, HEADS), ALU.mult).then_inc(tail_d, 1)
                    dve.tensor_copy(tail[:, :, :, 3 * HEADS], last).then_inc(tail_d, 1)
                    dve.wait_ge(tp1_d, ONE + n(1) + 1)
                    dve.wait_ge(tail_d, ONE + n(2) + 2)
                    dve.tensor_tensor(tails[:, 1], tails[:, 0], parts[0], ALU.subtract).then_inc(msum_d, 1)
                    dve.wait_ge(msum_d, ONE + n(2) + 1)
                    dve.tensor_copy(parts[1], tails[:, 1]).then_inc(tp2_d, 1)
                    dve.wait_ge(tp2_d, ONE + n(1) + 1)
                    dve.tensor_tensor(parts[2], tails[:, 1], parts[1], ALU.subtract).then_inc(tp3_d, 1)
                    dve.wait_ge(saved, ONE + n(SV))
                    dve.wait_ge(look_d, ONE + n(1))
                    settle(dve, settled)
                    build(1, *nxt)
                    for v in range(SV):
                        dve.tensor_copy(st[:, S1:S1 + 2 * flat].rearrange("p (s v) -> p s v", v=SV)[:, :, v:v + 1],
                                        K.state[:, bass.ds(blk[v], 1), :].rearrange("p o s -> p s o")).then_inc(loaded, 1)
                    dve.wait_ge(loaded, ONE + n(SV) + SV)
                    for _ in split(1, st[:, S2:S2 + flat], n):
                        pass
                    dve.wait_ge(sm_d, ONE + n(1) + 1)
                    pm = ps_m[:, 0:SV * NM].rearrange("p (v s) -> p v s", s=NM)
                    dve.tensor_reduce(zz[:, 2, :].rearrange("p (h v) -> p h v", v=SV),
                                      pm[:, :, 0:3 * HEADS].rearrange("p v (k h) -> p h v k", h=HEADS), AX, ALU.add).then_inc(msum_d, 1)
                    dve.tensor_scalar(gone[:].unsqueeze(2), pm[:, :, NM - 1:NM], -1.0, BIG, ALU.add, ALU.mult).then_inc(gone_d, 1)
                    dve.wait_ge(gone_d, ONE + n(1) + 2)
                    dve.wait_ge(msum_d, ONE + n(2) + 2)
                    dve.tensor_tensor(sv_[:].rearrange("p (h v) -> p h v", v=SV), hv(zz[:, 2, :], 0),
                                      bc(gone[:], 1, HEADS), ALU.add).then_inc(sv_d, 1)
                    dve.wait_ge(sv_d, ONE + n(1) + 1)
                    dve.tensor_tensor(sv_[:], sv_[:], st[:, S1:S1 + flat], ALU.max).then_inc(mx_d, 1)
                    dve.wait_ge(mx_d, ONE + n(1) + 1)
                    brk = K.brk[:, bass.ds(n(1), 1), :, :].rearrange("p o h v -> p (o h v)")
                    dve.tensor_tensor_scan(st[:, SN:SN + flat], brk, sv_[:], -BIG, ALU.add, ALU.max).then_inc(run_d, 1)
                    dve.wait_ge(run_d, ONE + n(1) + 1)
                    def save(v):
                        dve.wait_ge(saved, ONE + n(SV) + v)
                        dve.tensor_scalar(K.state[:, bass.ds(blk[v], 1), 0:HEADS].rearrange("p o s -> p s o"),
                                          hv(st, SN)[:, :, v:v + 1], 1.0, None, ALU.mult).then_inc(saved, 1)
                    dve.tensor_tensor(zz[:, 1, :], st[:, SN:SN + flat], st[:, S2:S2 + flat], ALU.add).then_inc(z1_d, 1)
                    dve.tensor_tensor(zz[:, 0, :], st[:, SN - 1:SN - 1 + flat], brk, ALU.add).then_inc(old1, 1)
                    dve.wait_ge(z1_d, ONE + n(1) + 1)
                    dve.scalar_tensor_tensor(zz[:, 1, :], zz[:, 1, :], SLOPE, zz[:, 1, :], ALU.mult, ALU.max).then_inc(lk1_d, 1)
                    dve.wait_ge(old1, ONE + n(1) + 1)
                    dve.tensor_tensor(zz[:, 0, :], zz[:, 0, :], st[:, S1:S1 + flat], ALU.max).then_inc(old_d, 1)
                    dve.wait_ge(lk1_d, ONE + n(1) + 1)
                    link = split(0, zz[:, 1, :], n)
                    next(link)
                    dve.wait_ge(old_d, ONE + n(1) + 1)
                    dve.tensor_tensor(zz[:, 0, :], zz[:, 0, :], st[:, S2:S2 + flat], ALU.add).then_inc(z_d, 1)
                    next(link)
                    dve.wait_ge(z_d, ONE + n(1) + 1)
                    dve.scalar_tensor_tensor(zz[:, 0, :], zz[:, 0, :], SLOPE, zz[:, 0, :], ALU.mult, ALU.max).then_inc(lk_d, 1)
                    next(link)
                    dve.wait_ge(lk_d, ONE + n(1) + 1)
                    dve.wait_ge(fo_d, ONE + n(1))
                    dve.tensor_tensor(zz[:, 3, :], zz[:, 0, :], zz[:, 1, :], ALU.subtract).then_inc(fa_d, 1)
                    next(link)
                    for v in range(SV):
                        save(v)
                    build(2, *nxt)
                    dve.wait_ge(look_d, ONE + n(1) + 1)
                    lk = ps_l[:, 0:SV * CH * 2 * HEADS].rearrange("p (v j s) -> p v j s", j=CH, s=2 * HEADS)
                    scv = sc[:].rearrange("p (v j h) -> p v j h", j=CH, h=HEADS)
                    dve.wait_ge(w_d, ONE + n(1))
                    dve.tensor_tensor(scv, xg[q][:, :, :, RW:TW], lk[:, :, :, HEADS:2 * HEADS], ALU.add).then_inc(s1_d, 1)
                    dve.wait_ge(s1_d, ONE + n(1) + 1)
                    dve.scalar_tensor_tensor(sc[:], sc[:], SLOPE, sc[:], ALU.mult, ALU.max).then_inc(s2_d, 1)
                    dve.wait_ge(s2_d, ONE + n(1) + 1)
                    dve.tensor_tensor(scv, scv, lk[:, :, :, 0:HEADS], ALU.subtract).then_inc(s3_d, 1)
                    dve.wait_ge(s3_d, ONE + n(1) + 1)
                    dve.tensor_scalar(sc[:], sc[:], 0.0, None, ALU.min).then_inc(s4_d, 1)
                    dve.wait_ge(w_d, ONE + n(1) + 1)
                    dve.wait_ge(fo_d, ONE + n(1) + 1)
                    for v in range(SV + 1):
                        if v < SV:
                            dve.wait_ge(py_d, ONE + n(SV) + max(v - 1, 0))
                            dve.tensor_tensor(y[v % 2][:, 0:YV].rearrange("p j (h c) -> p j h c", c=HC),
                                              xg[q][:, v, 0:YV, 0:RW].rearrange("p j (h c) -> p j h c", c=HC),
                                              bc(w[:, v * CH:v * CH + YV, :], 3, HC), ALU.mult).then_inc(y_d, 1)
                        if v == 1:
                            build(3, *nxt)
                        if v > 0:
                            scale(v - 1, blk[v - 1], n)
                            add_up(v - 1, blk[v - 1], n)

                def split(k, src, n):
                    part = [pair[:, t, k * HEADS:(k + 1) * HEADS, :].rearrange("p h v -> p (h v)") for t in range(3)]
                    rest, done = pair_rest[:, k, :], 8 if k == 0 else 4
                    yield dve.tensor_copy(part[0], src).then_inc(pp_d, 1)
                    dve.wait_ge(pp_d, ONE + n(8) + (done - 3))
                    yield dve.tensor_tensor(rest, src, part[0], ALU.subtract).then_inc(pp_d, 1)
                    dve.wait_ge(pp_d, ONE + n(8) + (done - 2))
                    yield dve.tensor_copy(part[1], rest).then_inc(pp_d, 1)
                    dve.wait_ge(pp_d, ONE + n(8) + (done - 1))
                    yield dve.tensor_tensor(part[2], rest, part[1], ALU.subtract).then_inc(pp_d, 1)

                def sums(blk):
                    return K.acc[:, bass.ds(blk, 1), :].rearrange("p o (h c) -> p (o h) c", c=HC)

                def scale(v, blk, n):
                    dve.wait_ge(acc_d, ONE + n(SV) + v)
                    dve.tensor_tensor(sums(blk), sums(blk), bc(hv(fo, 0)[:, :, v], 2, HC), ALU.mult).then_inc(sc_d, 1)

                def add_up(v, blk, n):
                    dve.wait_ge(sc_d, ONE + n(SV) + (v + 1))
                    dve.wait_ge(py_d, ONE + n(SV) + (v + 1))
                    dve.tensor_tensor(sums(blk), sums(blk), ps_y[v % 2][:, 0:RW].rearrange("p (h c) -> p h c", c=HC), ALU.add).then_inc(acc_d, 1)
                steps(dve, body)


def experts(nc, io, dr, K):
    with ExitStack() as ctx:
        m = Mem(nc, ctx)
        w1 = m.sb("w1", [P, 2, E, D])
        w2 = m.sb("w2", [P, 2, E, D])
        wo = m.sb("wo", [P, 2, E, D])
        h1 = m.sb("h1", [P, 2, IN_])
        h2 = m.sb("h2", [P, 2, IN_])
        zt = [m.sb(f"zt{q}", [P, 2, IN_]) for q in range(2)]
        yb = [m.sb(f"yb{q}", [P, IB, D]) for q in range(2)]
        x7 = m.sb("x7e", [P, IB, D])
        xnt7 = m.sb("xnt7e", [P, IB, 2, P])
        q7 = m.sb("q7", [P, IB, D])
        q2t7 = m.sb("q2t7", [P, IB, 2, P])
        wt7 = m.sb("wt7", [P, IB, P])
        wts = [m.sb(f"wts{q}", [P, IB, E]) for q in range(2)]
        lg = m.sb("lg", [P, IB, E])
        small = m.sb("small", [P, 10, IB])
        den = m.sb("den", [P, IB, HEADS])
        stats = m.sb("stats_e", [P, IB, 6])
        mv = m.sb("mv_e", [P, IB, 2])
        ps_h = [m.ps(f"ps_h{i}", [P, 512]) for i in range(4)]
        ps_y = [m.ps(f"ps_ye{i}", [P, 512]) for i in range(2)]
        ps_n = [m.ps(f"ps_n{i}", [P, 512]) for i in range(2)]
        w_in = [m.sem(f"experts_in{e}") for e in range(E)]
        x_in, xnt_in, out_d = m.sem("x_in_e"), m.sem("xnt_in"), m.sem("out_stored")
        names = """node_products node_reads hidden_products hidden_done expert_products expert_added
            q_biased q_squared q_fourth q_small1 q_small2 q_root q_small3 q_small4 q_small5 q_small6 q_scaled
            q_read z_based z_const den_done gat_done z_done stats_done_e aggr_done_e var_done_e std_done_e
            rstd_done_e zn_done zt_done lg_done lg_max lg_less lg_exp lg_sum lg_rec wts_done settled_e stored"""
        S = {k: m.count("s_" + k) for k in names.split()}
        NPR = 7 * IB
        HB = 8

        def stages(eng, node, expert):
            for k in range(7):
                node(k, 0, lambda c: 0, None)

            def iteration(q, t, more):
                for e in range(E):
                    expert(e, q, t)
                    if more and e < 7:
                        node(e, 1 - q, lambda c: t(c) + c, t)
            with eng.Fori(0, NI // 2) as i:
                for q in range(2):
                    iteration(q, lambda c, q=q, i=i: i * (2 * c) + q * c, True)
            iteration(0, lambda c: (NI - 1) * c, False)

        m.start_counts(((S["hidden_done"], 4),))
        with nc.Block() as block:
            @block.sync
            def _(sp):
                for e in range(E):
                    for dst, name in ((w1, "w1"), (w2, "w2"), (wo, "wo")):
                        sp.dma_start(dst[:, :, e, :], io[name][:, :, e, :]).then_inc(w_in[e], 16)

                def node(k, q, t, before):
                    if k == 0:
                        sp.wait_ge(S["node_products"], ONE + t(NPR))
                        sp.dma_start(x7[:], io["x"][bass.ds(t(IN_), IN_), :].rearrange("(j p) c -> p j c", p=P)).then_inc(x_in, 16)
                        sp.dma_start(xnt7[:].rearrange("p j k n -> p (j k n)"),
                                     dr["xnt"][bass.ds(t(1), 1)].rearrange("o p c -> (o p) c")).then_inc(xnt_in, 16)

                def expert(e, q, t):
                    if e == E - 1:
                        sp.wait_ge(S["expert_added"], ONE + t(E * IB) + E * IB)
                        sp.dma_start(io["out"][bass.ds(t(IN_), IN_), :].rearrange("(j p) c -> p j c", p=P), yb[q][:]).then_inc(out_d, 16)
                        sp.wait_ge(out_d, t(16) + 16)
                        sp.sem_inc(S["stored"], 1)
                stages(sp, node, expert)
                sp.wait_ge(out_d, 16 * NI)

            @block.tensor
            def _(pe):
                ident = K.cst[:, C_ID:C_ID + P]

                def node(k, q, t, before):
                    for j in range(IB):
                        f = k * IB + j
                        bank = ps_n[f % 2]
                        pe.wait_ge(S["node_reads"], ONE + t(NPR) + (f if j == 0 else f - 1))
                        if k == 0:
                            if j == 0:
                                pe.wait_ge(xnt_in, t(16) + 16)
                            for kh in range(2):
                                mm = pe.matmul(bank[:, 0:D], xnt7[:, j, kh, :], K.wq[:, kh, :], start=(kh == 0), stop=(kh == 1))
                        elif k == 1:
                            pe.wait_ge(S["q_scaled"], ONE + t(IB) + (j + 1))
                            for kh in range(2):
                                mm = pe.transpose(bank[:, kh * P:(kh + 1) * P], q7[:, j, kh * P:(kh + 1) * P], ident)
                        elif k == 2:
                            for kh in range(2):
                                pe.matmul(bank[:, 0:D], xnt7[:, j, kh, :], K.wvo[:, kh, :], start=(kh == 0), stop=False)
                            for kh in range(2):
                                mm = pe.matmul(bank[:, 0:D], q2t7[:, j, kh, :], K.kvw[:, kh, :], start=False, stop=(kh == 1))
                        elif k == 3:
                            pe.wait_ge(S["zn_done"], ONE + t(IB) + (j + 1))
                            for kh in range(2):
                                mm = pe.transpose(bank[:, kh * P:(kh + 1) * P], x7[:, j, kh * P:(kh + 1) * P], ident)
                        elif k == 4:
                            for kh in range(2):
                                mm = pe.matmul(bank[:, 0:E], zt[q][:, kh, j * P:(j + 1) * P], K.wr[:, kh, :], start=(kh == 0), stop=(kh == 1))
                        elif k == 5:
                            pe.wait_ge(S["wts_done"], ONE + t(1) + 1)
                            mm = pe.transpose(bank[0:E, 0:P], wts[q][:, j, :], ident)
                        else:
                            mm = pe.matmul(bank[:, 0:D], wt7[0:E, j, :], K.bo[0:E, :], start=True, stop=True)
                        mm.then_inc(S["node_products"], 1)

                def expert(e, q, t):
                    if e == 0:
                        pe.wait_ge(S["node_reads"], ONE + t(NPR) + NPR)
                    pe.wait_ge(w_in[e], 48)
                    done = t(E * HB) + (e * HB)
                    for layer in range(2):
                        wl, src = ((w1, zt[q]), (w2, h1))[layer]
                        for half in range(2):
                            for mh in range(2):
                                g = layer * 4 + half * 2 + mh
                                pe.wait_ge(S["hidden_done"], ONE + done + (g + 1))
                                if layer == 1 and mh == 0:
                                    pe.wait_ge(S["hidden_done"], ONE + done + (4 + half * 2 + 2))
                                for kh in range(2):
                                    mm = pe.matmul(ps_h[g % 4][:, 0:HN], wl[:, kh, e, mh * P:(mh + 1) * P],
                                                   src[:, kh, half * HN:(half + 1) * HN], start=(kh == 0), stop=(kh == 1))
                                mm.then_inc(S["hidden_products"], 1)
                    for j in range(IB):
                        if j in (0, HN // P):
                            pe.wait_ge(S["hidden_done"], ONE + done + (4 + 6 + (2 if j else 0)))
                        pe.wait_ge(S["expert_added"], ONE + t(E * IB) + (e * IB + max(j - 1, 0)))
                        for kh in range(2):
                            mm = pe.matmul(ps_y[j % 2][:, 0:D], h2[:, kh, j * P:(j + 1) * P], wo[:, kh, e, :],
                                           start=(kh == 0), stop=(kh == 1))
                        mm.then_inc(S["expert_products"], 1)
                stages(pe, node, expert)

            @block.scalar
            def _(act):
                def product(k, j, t):
                    act.wait_ge(S["node_products"], ONE + t(NPR) + (k * IB + j + 1))

                def node(k, q, t, before):
                    if k == 0:
                        for j in range(IB):
                            act.wait_ge(S["node_reads"], ONE + t(NPR) + (j + 1))
                            act.activation(q7[:, j, :], q7[:, j, :], ACT.Square, accum_out=small[:, 0, j:j + 1]).then_inc(S["q_squared"], 1)
                            act.wait_ge(S["q_squared"], ONE + t(IB) + (j + 1))
                            act.activation(q2t7[:, j, :, :].rearrange("p k n -> p (k n)"), q7[:, j, :], ACT.Square,
                                           accum_out=small[:, 1, j:j + 1]).then_inc(S["q_fourth"], 1)
                        act.wait_ge(S["q_fourth"], ONE + t(IB) + IB)
                        act.activation(small[:, 2, :], small[:, 1, :], ACT.Sqrt).then_inc(S["q_root"], 1)
                    elif k == 1:
                        for j in range(IB):
                            product(k, j, t)
                            act.copy(q2t7[:, j, :, :].rearrange("p k n -> p (k n)"), ps_n[(k * IB + j) % 2][:, 0:D]).then_inc(S["node_reads"], 1)
                    elif k == 2:
                        act.wait_ge(S["var_done_e"], ONE + t(1) + 1)
                        act.activation(small[:, 9, :], small[:, 8, :], ACT.Sqrt).then_inc(S["std_done_e"], 1)
                    elif k == 3:
                        for j in range(IB):
                            product(k, j, t)
                            act.copy(zt[q][:, :, j * P:(j + 1) * P], ps_n[(k * IB + j) % 2][:, 0:D].rearrange("p (k n) -> p k n", n=P)).then_inc(S["node_reads"], 1)
                    elif k == 4:
                        act.wait_ge(S["lg_less"], ONE + t(1) + 1)
                        act.activation(lg[:], lg[:], ACT.Exp).then_inc(S["lg_exp"], 1)
                    elif k == 5:
                        for j in range(IB):
                            product(k, j, t)
                            act.copy(wt7[0:E, j, :], ps_n[(k * IB + j) % 2][0:E, 0:P]).then_inc(S["node_reads"], 1)

                def expert(e, q, t):
                    done = t(E * HB) + (e * HB)
                    for layer in range(2):
                        for half in range(2):
                            for mh in range(2):
                                g = layer * 4 + half * 2 + mh
                                act.wait_ge(S["hidden_products"], ONE + done + (g + 1))
                                c = 2 * e + mh
                                act.activation((h1, h2)[layer][:, mh, half * HN:(half + 1) * HN], ps_h[g % 4][:, 0:HN],
                                               ACT.Relu, bias=K.bnb[:, layer, c:c + 1], scale=K.bns[:, layer, c:c + 1])\
                                   .then_inc(S["hidden_done"], 1)
                stages(act, node, expert)

            @block.vector
            def _(dve):
                def product(k, j, t):
                    dve.wait_ge(S["node_products"], ONE + t(NPR) + (k * IB + j + 1))

                def bank(k, j):
                    return ps_n[(k * IB + j) % 2]

                def step(name, t, ins):
                    ins.then_inc(S[name], 1)
                    dve.wait_ge(S[name], ONE + t(1) + 1)

                def node(k, q, t, before):
                    at = bass.ds(t(IB), IB)
                    if k == 0:
                        for j in range(IB):
                            product(k, j, t)
                            dve.tensor_tensor(q7[:, j, :], bank(k, j)[:, 0:D], K.bq[:], ALU.add).then_inc(S["node_reads"], 1)
                        dve.wait_ge(S["q_fourth"], ONE + t(IB) + IB)
                        step("q_small1", t, dve.tensor_scalar(small[:, 3, :], small[:, 0, :], DIV_EPS, None, ALU.add))
                        step("q_small2", t, dve.reciprocal(small[:, 4, :], small[:, 3, :]))
                        dve.wait_ge(S["q_root"], ONE + t(1) + 1)
                        step("q_small3", t, dve.tensor_tensor(small[:, 5, :], small[:, 2, :], small[:, 4, :], ALU.mult))
                        step("q_small4", t, dve.tensor_scalar(small[:, 6, :], small[:, 5, :], NORM_EPS, None, ALU.max))
                        step("q_small5", t, dve.reciprocal(small[:, 7, :], small[:, 6, :]))
                        step("q_small6", t, dve.tensor_tensor(small[:, 5, :], small[:, 7, :], small[:, 4, :], ALU.mult))
                        for j in range(IB):
                            dve.tensor_scalar(q7[:, j, :], q7[:, j, :], small[:, 5, j:j + 1], None, ALU.mult).then_inc(S["q_scaled"], 1)
                    elif k == 2:
                        dve.wait_ge(x_in, t(16) + 16)
                        if before:
                            dve.wait_ge(S["stored"], ONE + before(1))
                        step("den_done", t, dve.reciprocal(den[:].unsqueeze(3), K.acc[:, at, :].rearrange("p j (h c) -> p j h c", c=HC)[:, :, :, HD:HC]))
                        for j in range(IB):
                            product(k, j, t)
                            dve.tensor_tensor(yb[q][:, j, :], bank(k, j)[:, 0:D], x7[:, j, :], ALU.add).then_inc(S["node_reads"], 1)
                            a = K.acc[:, bass.ds(t(IB) + j, 1), :]
                            dve.tensor_tensor(q7[:, j, :].rearrange("p (h c) -> p h c", c=HD),
                                              a.rearrange("p o (h c) -> p (o h) c", c=HC)[:, :, 0:HD],
                                              bc(den[:, j, :], 2, HD), ALU.mult).then_inc(S["gat_done"], 1)
                            dve.wait_ge(S["node_reads"], ONE + t(NPR) + (k * IB + j + 1))
                            dve.tensor_tensor(yb[q][:, j, :], yb[q][:, j, :], K.cb[:], ALU.add).then_inc(S["z_const"], 1)
                            dve.wait_ge(S["gat_done"], ONE + t(IB) + (j + 1))
                            dve.wait_ge(S["z_const"], ONE + t(IB) + (j + 1))
                            dve.scalar_tensor_tensor(yb[q][:, j, :], q7[:, j, :], 0.0, yb[q][:, j, :], ALU.max, ALU.add).then_inc(S["z_done"], 1)
                            if j > 0:
                                dve.bn_stats(stats[:, j - 1, :], yb[q][:, j - 1, :]).then_inc(S["stats_done_e"], 1)
                        dve.wait_ge(S["z_done"], ONE + t(IB) + IB)
                        dve.bn_stats(stats[:, IB - 1, :], yb[q][:, IB - 1, :]).then_inc(S["stats_done_e"], 1)
                        dve.wait_ge(S["stats_done_e"], ONE + t(IB) + IB)
                        settle(dve, S["settled_e"])
                        for j in range(IB):
                            dve.bn_aggr(mv[:, j, :], stats[:, j, :]).then_inc(S["aggr_done_e"], 1)
                        dve.wait_ge(S["aggr_done_e"], ONE + t(IB) + IB)
                        dve.tensor_scalar(small[:, 8, :].unsqueeze(2), mv[:, :, 1:2], LN_EPS, None, ALU.add).then_inc(S["var_done_e"], 1)
                        dve.wait_ge(S["std_done_e"], ONE + t(1) + 1)
                        step("rstd_done_e", t, dve.reciprocal(small[:, 9, :], small[:, 9, :]))
                        for j in range(IB):
                            dve.tensor_scalar(x7[:, j, :], yb[q][:, j, :], mv[:, j, 0:1], small[:, 9, j:j + 1],
                                              ALU.subtract, ALU.mult).then_inc(S["zn_done"], 1)
                    elif k == 4:
                        for j in range(IB):
                            product(k, j, t)
                            dve.tensor_tensor(lg[:, j, :], bank(k, j)[:, 0:E], K.br[:], ALU.add).then_inc(S["node_reads"], 1)
                        dve.wait_ge(S["node_reads"], ONE + t(NPR) + (k + 1) * IB)
                        step("lg_max", t, dve.tensor_reduce(small[:, 3, :], lg[:], AX, ALU.max))
                        dve.tensor_tensor(lg[:], lg[:], bc(small[:, 3, :], 2, E), ALU.subtract).then_inc(S["lg_less"], 1)
                        dve.wait_ge(S["lg_exp"], ONE + t(1) + 1)
                        step("lg_sum", t, dve.tensor_reduce(small[:, 4, :], lg[:], AX, ALU.add))
                        step("lg_rec", t, dve.reciprocal(small[:, 6, :], small[:, 4, :]))
                        dve.tensor_tensor(wts[q][:], lg[:], bc(small[:, 6, :], 2, E), ALU.mult).then_inc(S["wts_done"], 1)
                    elif k == 6:
                        for j in range(IB):
                            product(k, j, t)
                            dve.tensor_tensor(yb[q][:, j, :], yb[q][:, j, :], bank(k, j)[:, 0:D], ALU.add).then_inc(S["node_reads"], 1)

                def expert(e, q, t):
                    if e == 0:
                        dve.wait_ge(S["node_reads"], ONE + t(NPR) + NPR)
                    dve.wait_ge(S["expert_added"], ONE + t(E * IB) + e * IB)
                    for j in range(IB):
                        dve.wait_ge(S["expert_products"], ONE + t(E * IB) + (e * IB + j + 1))
                        dve.scalar_tensor_tensor(yb[q][:, j, :], ps_y[j % 2][:, 0:D], wts[q][:, j, e:e + 1], yb[q][:, j, :],
                                                 ALU.mult, ALU.add).then_inc(S["expert_added"], 1)
                stages(dve, node, expert)


def graph_layer(nc, io):
    with ExitStack() as ctx:
        m = Mem(nc, ctx)
        Mem.sems = []
        dr = {"src": nc.dram_tensor("list_src", [LROWS, GE], I32).ap(),
              "dst": nc.dram_tensor("list_dst", [LROWS, GE], I32).ap(),
              "table": nc.dram_tensor("edge_table", [NPAD, TW], F32).ap(),
              "xnt": nc.dram_tensor("xn_turned", [NI, P, IB * D], F32).ap()}

        class K:
            cst = m.sb("cst", [P, C_W])
            cstb = m.sb("cstb", [P, 2 * P], BF16)
            acc = m.sb("acc", [P, NB, RW])
            state = m.sb("state", [P, NB, 2 * HEADS])
            wq, wvo, kvw = (m.sb(n, [P, 2, D]) for n in ("wq", "wvo", "kvw"))
            bq, cb = (m.sb(n, [P, D]) for n in ("bq", "cb"))
            bns, bnb = (m.sb(n, [P, 2, 2 * E]) for n in ("bns", "bnb"))
            wr, br, bo = m.sb("wr", [P, 2, E]), m.sb("br", [P, E]), m.sb("bo", [E, D])
        with ExitStack() as lists:
            ml = Mem(nc, lists)
            K.rel = ml.sb("rel", [P, NVT * CH], BF16)
            K.last = ml.sb("last", [P, NVT * CH], BF16)
            K.ix = ml.sb("ix", [P, NVT * CH], I32)
            K.brk = ml.sb("brk", [P, NVT // SV, HEADS, SV], BF16)
            K.blk = ml.sb("blk", [1, NVT // 4], I32)
            edge_lists(nc, io, dr, K)
            with ExitStack() as early:
                me = Mem(nc, early)
                K.wcat = me.sb("wcat", [P, 2, D + 2 * HEADS])
                K.wk, K.bk, K.bvw = me.sb("wk", [P, 2, D]), me.sb("bk", [P, D]), me.sb("bvw", [P, D])
                weights(nc, io, K)
                project(nc, io, dr, K)
            Mem.clear(nc)
            attend(nc, dr, K)
        experts(nc, io, dr, K)


def kernel(**inputs):
    import concourse.bacc as bacc
    from concourse.bass_utils import run_bass_kernel_spmd as run

    a = {k: np.asarray(v) for k, v in inputs.items()}

    def rows(w):
        return np.ascontiguousarray(w.reshape(2, P, -1).transpose(1, 0, 2))

    def expert_rows(w):
        return np.ascontiguousarray(w.reshape(E, 2, P, D).transpose(2, 1, 0, 3))

    def channels(v):
        return v.reshape(E, 2, P).transpose(2, 0, 1).reshape(P, 2 * E)

    def edges(v, fill):
        out = np.full(LROWS * GE, fill, v.dtype)
        out[:EDGES] = v
        return out.reshape(LROWS, GE)

    x = np.zeros((NPAD, D), a["x"].dtype)
    x[:N] = a["x"]
    cst = np.zeros((P, C_W), np.float32)
    cst[:, C_ID:C_ID + P] = np.eye(P)
    cst[:, C_IOTA:C_IOTA + P] = np.arange(P)
    cst[:, C_VALID:C_VALID + NB] = np.arange(NB) * P + np.arange(P)[:, None] < N
    cst[:, C_GLAST] = np.arange(P) % CH == CH - 1
    cst[:, C_THR] = np.arange(P) * P
    cst_row = np.zeros((1, NVT), np.float32)
    cst_row[0, NG:NG + NX] = np.arange(1, NB)
    f = {k: a["L0_ffn_" + k] for k in ("b1", "g1", "be1", "m1", "v1", "b2", "g2", "be2", "m2", "v2")}
    given = {
        "x": x, "src": edges(a["src"], 0), "dst": edges(a["dst"], NODST), "cst": cst, "cst_row": cst_row,
        "firsts": np.ascontiguousarray(a["dst"][::GE].reshape(1, NG)),
        "w_gat": rows(a["L0_gnn_W"]), "att_src": a["L0_gnn_att_src"].reshape(D), "att_dst": a["L0_gnn_att_dst"].reshape(D),
        "w_qkv": rows(a["L0_mix_W_qkv"]), "b_qkv": a["L0_mix_b_qkv"],
        "bv_col": np.ascontiguousarray(a["L0_mix_b_qkv"][2 * D:].reshape(2, P).T),
        "w_out": rows(a["L0_mix_W_out"]), "b_out": a["L0_mix_b_out"],
        "w_r": rows(a["L0_ffn_Wr"]), "b_r": a["L0_ffn_br"], "b_o": a["L0_ffn_bo"],
        "w1": expert_rows(a["L0_ffn_W1"]), "w2": expert_rows(a["L0_ffn_W2"]), "wo": expert_rows(a["L0_ffn_Wo"]),
        "bn": np.stack([channels(f[n + i]) for n in ("b", "g", "be", "m", "v") for i in "12"], axis=1),
    }
    nc = bacc.Bacc("TRN2", target_bir_lowering=False, num_devices=1)
    io = {k: nc.dram_tensor(f"in_{k}", v.shape, mybir.dt.from_np(v.dtype), kind="ExternalInput").ap()
          for k, v in given.items()}
    io["out"] = nc.dram_tensor("out_x", (NPAD, D), F32, kind="ExternalOutput").ap()
    graph_layer(nc, io)
    r = run(nc, [{f"in_{k}": v for k, v in given.items()}], core_ids=[0])
    return r.results[0]["out_x"][:N]
```

```python
from contextlib import ExitStack

import numpy as np

import concourse.bass as bass
from concourse import mybir

ALU = mybir.AluOpType
ACT = mybir.ActivationFunctionType
AX = mybir.AxisListType.X
F32 = mybir.dt.float32
BF16 = mybir.dt.bfloat16
I32 = mybir.dt.int32

P = 128
N, D = 6250, 256
HEADS, HD = 4, 64
NB = -(-N // P)
NPAD = NB * P
EDGES = 200000
CH = 4
GE = CH * P
NG = -(-EDGES // GE)
NX = NB - 1
SV = 8
NS = -(-(NG + NX) // SV)
NVT = 448
TT = NVT * CH // P
LROWS = NVT + 1
NODST = 7000
BIG = 1.0e34
HC = HD + 1
RW = HEADS * HC
TW = RW + HEADS
MW = 2 * D + 2
E, LN_EPS, BN_EPS, DIV_EPS, NORM_EPS = 8, 1e-5, 1e-3, 1e-7, 1e-12
IB = 7
NI = NB // IB
IN_ = IB * P
HN = IN_ // 2
SLOPE = 0.2
ONE = 1

C_ID, C_IOTA, C_VALID, C_GLAST, C_THR, C_W = 0, P, 2 * P, 2 * P + NB, 2 * P + NB + 1, 2 * P + NB + 2


def bc(ap, axis, n):
    a = ap.unsqueeze(axis)
    shape = list(a.shape)
    shape[axis] = n
    return a.to_broadcast(shape)


def chain(eng, sem):
    n = [0]

    def link(ins):
        n[0] += 1
        ins.then_inc(sem, 1)
        eng.wait_ge(sem, ONE + n[0])
    return link


def settle(eng, sem):
    eng.sem_inc(sem, 1)


class Mem:

    sems = []

    def __init__(self, nc, ctx):
        self.nc, self.ctx, self.counts = nc, ctx, []

    def sb(self, name, shape, dt=F32):
        return self.ctx.enter_context(self.nc.sbuf_tensor(name, shape, dt))

    def ps(self, name, shape, dt=F32):
        return self.ctx.enter_context(self.nc.psum_tensor(name, shape, dt))

    def sem(self, name):
        Mem.sems.append(self.nc.alloc_semaphore(name=name))
        return Mem.sems[-1]

    def count(self, name):
        self.counts.append(self.sem(name))
        return self.counts[-1]

    def start_counts(self, ahead=()):
        with self.nc.Block() as block:
            @block.gpsimd
            def _(pool):
                for c in self.counts:
                    pool.sem_inc(c, ONE)
                for c, n in ahead:
                    pool.sem_inc(c, n)

    @staticmethod
    def clear(nc):
        nc.clear_and_free_semaphores(Mem.sems)
        nc.all_engine_barrier()
        Mem.sems = []


class Given:

    def __init__(self, m, io, K):
        self.wqkv = m.sb("wqkv", [P, 2, 3 * D])
        self.bqkv = m.sb("bqkv", [P, 3 * D])
        self.wout = m.sb("wout", [P, 2, D])
        self.bout = m.sb("bout", [P, D])
        self.bvc = m.sb("bvc", [P, 2])
        self.att = m.sb("att", [P, 2, D])
        self.bnp = m.sb("bnp", [P, 10, 2 * E])
        self.loaded = m.sem("w_in")
        self.loads = ((self.wqkv[:], io["w_qkv"]), (self.wout[:], io["w_out"]), (self.bvc[:], io["bv_col"]),
                      (self.bqkv[:], io["b_qkv"].partition_broadcast(P)),
                      (self.bout[:], io["b_out"].partition_broadcast(P)),
                      (self.att[:, 0, :], io["att_src"].partition_broadcast(P)),
                      (self.att[:, 1, :], io["att_dst"].partition_broadcast(P)),
                      (K.wcat[:, :, 0:D], io["w_gat"]), (self.bnp[:], io["bn"]),
                      (K.wr[:], io["w_r"]), (K.br[:], io["b_r"].partition_broadcast(P)))


def edge_lists(nc, io, dr, K, W):
    with ExitStack() as ctx:
        m = Mem(nc, ctx)
        first_i = m.sb("first_i", [1, NG], I32)
        row = m.sb("row", [1, NVT])
        blkf = m.sb("blkf", [1, NVT])
        base = m.sb("base", [1, NVT])
        brk = m.sb("brk_row", [1, NVT])
        pack = m.sb("pack", [1, NVT // 4])
        ones = m.sb("ones_l", [P, P])
        below = m.sb("below", [P, NG])
        cnt = m.sb("cnt", [P, 3])
        gidx = m.sb("gidx", [P, 1], I32)
        xrows = m.sb("xrows", [P, 2, GE], I32)
        base_bc = m.sb("base_bc", [P, NVT])
        raw = m.sb("raw", [P, 3, TT, P], I32)
        rawf = [m.sb(f"rawf{q}", [P, 3, P]) for q in range(2)]
        ps_row = m.ps("ps_row", [P, 512])
        ps_pen = m.ps("ps_pen", [P, 512])
        ps_base = m.ps("ps_base", [P, 512])
        ps_brk = m.ps("ps_brk", [P, 512])
        ps_t = [m.ps(f"ps_t{i}", [P, 512]) for i in range(2)]
        consts_in, first_in, copied, gathered, extra_in = map(m.sem, (
            "consts_in", "first_in", "lists_copied", "extra_gathered", "extra_stored"))
        firsts_f, first_bc, idx_ready, pen_t, rows_ready, rows_bc, base_ready = map(m.count, (
            "firsts_f", "first_bc", "idx_ready", "pen_t", "rows_ready", "rows_bc", "base_ready"))
        tile_in = m.sem("tile_in")
        dch, ones_set, cast, turned, spread = map(m.count, (
            "dve_chain_l", "ones_set_l", "tile_cast", "tile_turned", "tile_spread"))

        m.start_counts(((spread, 3),))
        with nc.Block() as block:
            @block.sync
            def _(sp):
                sp.dma_start(K.cst[:], io["cst"]).then_inc(consts_in, 16)
                sp.dma_start(row[:], io["cst_row"]).then_inc(consts_in, 16)
                sp.dma_start(first_i[:], io["firsts"]).then_inc(first_in, 16)
                for name in ("src", "dst"):
                    sp.dma_start(dr[name][0:NG, :], io[name][0:NG, :]).then_inc(copied, 16)
                    sp.dma_start(dr[name][NG + NX:LROWS, :], io[name][NG + NX:LROWS, :]).then_inc(copied, 16)
                sp.wait_ge(gathered, 32)
                for k, name in enumerate(("src", "dst")):
                    sp.dma_start(dr[name][NG:NG + NX, :], xrows[1:1 + NX, k, :]).then_inc(extra_in, 16)
                sp.wait_ge(copied, 64)
                sp.wait_ge(extra_in, 32)
                flat = {k: dr[k].rearrange("g e -> (g e)") for k in ("src", "dst")}
                for k, (name, ahead) in enumerate((("dst", 0), ("dst", 1), ("src", 0))):
                    sp.dma_start(raw[:, k, :, :], flat[name][ahead:ahead + TT * P * P]
                                 .rearrange("(t p e) -> p t e", p=P, e=P)).then_inc(tile_in, 16)

            @block.scalar
            def _(act):
                for dst, src in W.loads:
                    act.dma_start(dst, src).then_inc(W.loaded, 16)

            @block.gpsimd
            def _(pool):
                pool.wait_ge(idx_ready, ONE + 1)
                for k, name in enumerate(("src", "dst")):
                    pool.indirect_dma_start(xrows[:, k, :], None, io[name],
                                            bass.IndirectOffsetOnAxis(ap=gidx[:, 0:1], axis=0)).then_inc(gathered, 16)

            @block.tensor
            def _(pe):
                pe.wait_ge(ones_set, ONE + 1)
                pe.wait_ge(firsts_f, ONE + 1)
                pe.matmul(ps_row[:, 0:NG], ones[0:1, :], base[0:1, 0:NG], start=True, stop=True).then_inc(first_bc, 1)
                pe.wait_ge(idx_ready, ONE + 1)
                pe.transpose(ps_pen[0:1, 0:P], cnt[:, 2:3], K.cst[:, C_ID:C_ID + P]).then_inc(pen_t, 1)
                pe.wait_ge(rows_ready, ONE + 1)
                pe.matmul(ps_base[:, 0:NVT], ones[0:1, :], base[0:1, :], start=True, stop=True).then_inc(rows_bc, 1)
                pe.matmul(ps_brk[:, 0:NVT], ones[0:1, :], brk[0:1, :], start=True, stop=True).then_inc(rows_bc, 1)
                with pe.Fori(0, TT // 2) as i:
                    for q in range(2):
                        pe.wait_ge(cast, ONE + i * 8 + (4 * q + 4))
                        pe.wait_ge(spread, ONE + i * 6 + 3 * q)
                        for k in range(3):
                            pe.transpose(ps_t[q][:, k * P:(k + 1) * P], rawf[q][:, k, :],
                                         K.cst[:, C_ID:C_ID + P]).then_inc(turned, 1)

            @block.vector
            def _(dve):
                link = chain(dve, dch)
                dve.memset(ones[:], 1.0).then_inc(ones_set, 1)
                link(dve.memset(blkf[:], 0.0))
                dve.wait_ge(first_in, 16)
                dve.tensor_copy(base[0:1, 0:NG], first_i[:]).then_inc(firsts_f, 1)
                link(dve.tensor_scalar(first_i[:], first_i[:], 7, None, ALU.arith_shift_right))
                link(dve.tensor_copy(blkf[0:1, 0:NG], first_i[:]))
                dve.wait_ge(consts_in, 32)
                link(dve.tensor_copy(blkf[0:1, NG:NG + NX], row[0:1, NG:NG + NX]))
                link(dve.tensor_copy(K.cstb[:], K.cst[:, 0:2 * P]))
                dve.wait_ge(first_bc, ONE + 1)
                link(dve.tensor_scalar(below[:], ps_row[:, 0:NG], K.cst[:, C_THR:C_THR + 1], None, ALU.is_lt))
                link(dve.tensor_reduce(cnt[:, 0:1], below[:], AX, ALU.add))
                link(dve.tensor_scalar(cnt[:, 1:2], cnt[:, 0:1], -1.0, 0.0, ALU.add, ALU.max))
                link(dve.tensor_scalar(cnt[:, 2:3], cnt[:, 0:1], 0.0, -1.0e6, ALU.is_equal, ALU.mult))
                dve.tensor_copy(gidx[:], cnt[:, 1:2]).then_inc(idx_ready, 1)
                dve.wait_ge(pen_t, ONE + 1)
                link(dve.tensor_scalar(base[:], blkf[:], float(P), None, ALU.mult))
                link(dve.tensor_tensor(base[0:1, NG:NG + NX], base[0:1, NG:NG + NX], ps_pen[0:1, 1:1 + NX], ALU.add))
                link(dve.memset(brk[:], 0.0))
                link(dve.tensor_tensor(brk[0:1, 1:NVT], blkf[0:1, 1:NVT], blkf[0:1, 0:NVT - 1], ALU.is_equal))
                link(dve.memset(brk[0:1, 0:NVT:SV], 0.0))
                link(dve.tensor_scalar(brk[:], brk[:], -1.0, BIG, ALU.add, ALU.mult))
                dve.engine_nop().then_inc(rows_ready, 1)
                b4 = blkf[:].rearrange("p (a b) -> p a b", b=4)
                pk = pack[:].unsqueeze(2)
                link(dve.scalar_tensor_tensor(pk, b4[:, :, 3:4], 64.0, b4[:, :, 2:3], ALU.mult, ALU.add))
                link(dve.scalar_tensor_tensor(pk, pk, 64.0, b4[:, :, 1:2], ALU.mult, ALU.add))
                link(dve.scalar_tensor_tensor(K.blk[:].unsqueeze(2), pk, 64.0, b4[:, :, 0:1], ALU.mult, ALU.add))
                dve.wait_ge(rows_bc, ONE + 2)
                dve.tensor_copy(base_bc[:], ps_base[:, 0:NVT]).then_inc(base_ready, 1)
                dve.tensor_copy(K.brk[:], bc(ps_brk[:, 0:NVT].rearrange("p (s v) -> p s v", v=SV), 2, HEADS))\
                   .then_inc(base_ready, 1)
                dve.wait_ge(base_ready, ONE + 2)
                dve.wait_ge(tile_in, 48)

                def casts(q, i, k):
                    tile = [raw[:, c, bass.ds(i * 2 + k, 1), :].rearrange("p o e -> p (o e)") for c in range(3)]
                    dve.tensor_tensor(rawf[q][:, 2, :], tile[0], tile[1], ALU.not_equal).then_inc(cast, 1)
                    dve.tensor_copy(rawf[q][:, 0, :], tile[0]).then_inc(cast, 1)
                    dve.tensor_copy(rawf[q][:, 1, :], tile[2]).then_inc(cast, 1)
                    dve.wait_ge(cast, ONE + i * 8 + (4 * k + 1))
                    dve.tensor_tensor(rawf[q][:, 2, P - 1:P], rawf[q][:, 2, P - 1:P], K.cst[:, C_GLAST:C_GLAST + 1],
                                      ALU.max).then_inc(cast, 1)

                def spreads(q, i):
                    dve.wait_ge(turned, ONE + i * 6 + (3 * q + 3))
                    at = bass.ds(i * (2 * P) + q * P, P)
                    dve.tensor_tensor(K.rel[:, at].rearrange("p (v j) -> p v j", j=CH),
                                      ps_t[q][:, 0:P].rearrange("p (v j) -> p v j", j=CH),
                                      bc(base_bc[:, bass.ds(i * (2 * P // CH) + q * (P // CH), P // CH)], 2, CH),
                                      ALU.subtract).then_inc(spread, 1)
                    dve.tensor_copy(K.ix[:, at], ps_t[q][:, P:2 * P]).then_inc(spread, 1)
                    dve.tensor_copy(K.last[:, at], ps_t[q][:, 2 * P:3 * P]).then_inc(spread, 1)
                casts(0, 0, 0)
                with dve.Fori(0, TT // 2 - 1) as i:
                    for q in range(2):
                        casts(1 - q, i, q + 1)
                        spreads(q, i)
                casts(1, TT // 2 - 1, 1)
                spreads(0, TT // 2 - 1)
                spreads(1, TT // 2 - 1)


def weights(nc, K, W):
    with ExitStack() as ctx:
        m = Mem(nc, ctx)
        wqkv, bqkv, wout, bout, bvc, att, bnp, w_in = W.wqkv, W.bqkv, W.wout, W.bout, W.bvc, W.att, W.bnp, W.loaded
        bvr = m.sb("bvr", [P, 2, P])
        prod = m.sb("prod", [P, 2, D])
        mean = m.sb("mean_w", [P, 6])
        std = m.sb("bn_std", [P, 2, 2 * E])
        wvt = m.sb("wvt", [P, 2, 2, P])
        ps = [m.ps(f"ps_w{i}", [P, 512]) for i in range(5)]
        bq_ready, bq_turned, dch, turned, wvt_ready, wvo, bvw, bvr_ready, var_ready, std_ready = map(m.count, (
            "bq_ready", "bq_turned",
            "dve_chain_w", "wv_turned", "wvt_ready", "wvo_done", "bvw_done", "bvr_ready", "bn_var", "bn_std"))
        m.start_counts()
        with nc.Block() as block:
            @block.scalar
            def _(act):
                act.wait_ge(var_ready, ONE + 1)
                act.activation(std[:], bnp[:, 8:10, :], ACT.Sqrt).then_inc(std_ready, 1)

            @block.tensor
            def _(pe):
                pe.wait_ge(w_in, len(W.loads) * 16)
                for ch in range(2):
                    for kh in range(2):
                        pe.transpose(ps[ch][:, kh * P:(kh + 1) * P],
                                     wqkv[:, kh, 2 * D + ch * P:2 * D + (ch + 1) * P],
                                     K.cst[:, C_ID:C_ID + P]).then_inc(turned, 1)
                pe.wait_ge(wvt_ready, ONE + 2)
                for mh in range(2):
                    for ch in range(2):
                        pe.matmul(ps[2][:, mh * D:(mh + 1) * D], wvt[:, ch, mh, :], wout[:, ch, :],
                                  start=(ch == 0), stop=(ch == 1)).then_inc(wvo, 1)
                pe.wait_ge(bvr_ready, ONE + 1)
                for ch in range(2):
                    pe.matmul(ps[3][:, 0:D], bvr[:, ch, :], wout[:, ch, :],
                              start=(ch == 0), stop=(ch == 1)).then_inc(bvw, 1)
                pe.wait_ge(bq_ready, ONE + 1)
                for kh in range(2):
                    pe.transpose(ps[4][:, kh * P:(kh + 1) * P], K.bq[:, kh * P:(kh + 1) * P],
                                 K.cst[:, C_ID:C_ID + P]).then_inc(bq_turned, 1)

            @block.vector
            def _(dve):
                link = chain(dve, dch)
                dve.wait_ge(w_in, len(W.loads) * 16)
                for kh in range(2):
                    for a in range(2):
                        link(dve.tensor_tensor(prod[:, a, :], K.wcat[:, kh, 0:D], att[:, a, :], ALU.mult))
                    for a in range(2):
                        link(dve.tensor_reduce(K.wcat[:, kh, D + 4 * a:D + 4 * a + 4],
                                               prod[:, a, :].rearrange("p (h c) -> p h c", c=HD), AX, ALU.add))
                for i in range(2):
                    link(dve.tensor_reduce(mean[:, 3 * i:3 * i + 2], wqkv[:, :, i * D:(i + 1) * D], AX, ALU.add))
                    link(dve.tensor_reduce(mean[:, 3 * i + 2:3 * i + 3], bqkv[:, i * D:(i + 1) * D], AX, ALU.add))
                link(dve.tensor_scalar(mean[:], mean[:], 1.0 / D, None, ALU.mult))
                for i, (w, b) in enumerate(((K.wq, K.bq), (K.wk, K.bk))):
                    for kh in range(2):
                        link(dve.tensor_scalar(w[:, kh, :], wqkv[:, kh, i * D:(i + 1) * D],
                                               mean[:, 3 * i + kh:3 * i + kh + 1], None, ALU.subtract))
                    link(dve.tensor_scalar(b[:], bqkv[:, i * D:(i + 1) * D],
                                           mean[:, 3 * i + 2:3 * i + 3], None, ALU.subtract))
                dve.engine_nop().then_inc(bq_ready, 1)
                dve.tensor_copy(bvr[:], bc(bvc[:], 2, P)).then_inc(bvr_ready, 1)
                link(dve.tensor_scalar(bnp[:, 8:10, :], bnp[:, 8:10, :], BN_EPS, None, ALU.add))
                dve.engine_nop().then_inc(var_ready, 1)
                dve.wait_ge(std_ready, ONE + 1)
                link(dve.reciprocal(std[:], std[:]))
                link(dve.tensor_tensor(K.bns[:], bnp[:, 2:4, :], std[:], ALU.mult))
                link(dve.tensor_tensor(bnp[:, 0:2, :], bnp[:, 0:2, :], bnp[:, 6:8, :], ALU.subtract))
                link(dve.tensor_tensor(bnp[:, 0:2, :], bnp[:, 0:2, :], K.bns[:], ALU.mult))
                link(dve.tensor_tensor(K.bnb[:], bnp[:, 0:2, :], bnp[:, 4:6, :], ALU.add))
                dve.wait_ge(turned, ONE + 4)
                for ch in range(2):
                    dve.tensor_copy(wvt[:, ch, :, :], ps[ch][:, 0:D].rearrange("p (a b) -> p a b", b=P)).then_inc(wvt_ready, 1)
                dve.wait_ge(wvo, ONE + 4)
                link(dve.tensor_copy(K.wvo[:], ps[2][:].rearrange("p (a b) -> p a b", b=D)))
                dve.wait_ge(bvw, ONE + 2)
                link(dve.tensor_copy(K.bvw[:], ps[3][:, 0:D]))
                link(dve.tensor_tensor(K.cb[:], K.bvw[:], bout[:], ALU.add))
                dve.wait_ge(bq_turned, ONE + 2)
                link(dve.tensor_copy(K.bqc[:], ps[4][:, 0:2 * P:P]))


def project(nc, io, dr, K):
    with ExitStack() as ctx:
        m = Mem(nc, ctx)
        x7 = [m.sb(f"x7_{q}", [P, IB, D]) for q in range(2)]
        xn7 = [m.sb(f"xn7_{q}", [P, IB, D]) for q in range(2)]
        xnt7 = [m.sb(f"xnt7_{q}", [P, IB, 2, P]) for q in range(2)]
        rows7 = [m.sb(f"rows7_{q}", [P, IB, RW + 2 * HEADS]) for q in range(2)]
        k7 = m.sb("k7", [P, IB, D])
        ks7 = m.sb("ks7", [P, 3, IB])
        kk7 = m.sb("kk7", [P, IB, D])
        k_acc, kk_acc = m.sb("k_acc", [P, IB, D]), m.sb("kk_acc", [P, IB, D])
        col = m.sb("col_sums", [P, 2, D])
        stats = m.sb("stats", [P, IB, 6])
        mv = m.sb("mv", [P, IB, 2])
        var = m.sb("var", [P, 2, IB])
        ones = m.sb("ones_p", [P, 2])
        zeros = m.sb("zeros_p", [P, 512])
        att = m.sb("at_sb", [P, 2, D])
        ssb = m.sb("s_sb", [P, 8])
        ps_t = [m.ps(f"ps_xt{i}", [P, 512]) for i in range(2)]
        ps_p = [m.ps(f"ps_p{i}", [P, 512]) for i in range(2)]
        ps_k = [m.ps(f"ps_k{i}", [P, 512]) for i in range(2)]
        ps_a = m.ps("ps_a", [P, 512])
        ps_s = m.ps("ps_s", [P, 512])
        settled = m.count("settled_p")
        pad_stored = m.sem("pad_stored")
        x_in, xnt_stored, rows_stored = ([m.sem(f"{n}{q}") for q in range(2)] for n in ("x_in", "xnt_stored", "rows_stored"))
        (set_, stats_d, aggr_d, var_d, std_d, rstd_d, xn_d, turned, xnt_d, proj_d, k_d, rows_d, kb_d, k2_d,
         r1_d, r2_d, r3_d, kn_d, kk_d, sums_d, init_d, fin, dch, end_sq, end_mm, added, col_d, col_mm) = map(m.count, (
            "consts_set_p", "stats_done", "aggr_done", "var_done", "std_done", "rstd_done", "xn_done", "x_turned",
            "xnt_done", "proj_done", "k_done", "rows_done", "k_biased", "k_squared", "r1_done", "r2_done", "r3_done",
            "k_normed", "k_fourth", "sums_done", "state_set", "all_summed", "dve_chain_p", "end_sqrt", "end_mm",
            "k_added", "columns_reduced", "columns_summed"))

        def pipeline(eng, front, back):
            def zero(c):
                return 0
            front(0, zero, zero)
            with eng.Fori(0, NI // 2) as i:
                for q in range(2):
                    t = lambda c, q=q, i=i: i * (2 * c) + q * c
                    u = lambda c, i=i: i * c
                    back(q, t, u, (1 - q, lambda c, t=t: t(c) + c, lambda c, q=q, i=i: i * c + q * c))
            back(0, lambda c: (NI - 1) * c, lambda c: (NI // 2) * c, None)

        m.start_counts([(s, 16) for s in xnt_stored + rows_stored])
        with nc.Block() as block:
            @block.sync
            def _(sp):
                def load(q, at):
                    sp.dma_start(x7[q][:], io["x"][bass.ds(at, IN_), :].rearrange("(j p) c -> p j c", p=P)).then_inc(x_in[q], 16)

                def store(q, i, f):
                    sp.wait_ge(xnt_d, ONE + i * (2 * IB) + (f + 1) * IB)
                    sp.dma_start(dr["xnt"][bass.ds(i * (2 * IB) + f * IB, IB)].rearrange("j p c -> p j c"),
                                 xnt7[q][:].rearrange("p j k n -> p j (k n)")).then_inc(xnt_stored[q], 16)
                load(0, 0)
                load(1, IN_)
                sp.wait_ge(set_, ONE + 4)
                pads = range(NB, NS, 2)
                for b in pads:
                    n = min(2, NS - b)
                    sp.dma_start(dr["xnt"][b:b + n].rearrange("j p c -> p j c"),
                                 zeros[:, 0:n * D].rearrange("p (j c) -> p j c", c=D)).then_inc(pad_stored, 16)
                store(0, 0, 0)
                with sp.Fori(0, (NI - 3) // 2) as i:
                    for q in range(2):
                        sp.wait_ge(xn_d, ONE + i * (2 * IB) + (q + 1) * IB)
                        load(q, i * (2 * IN_) + (q + 2) * IN_)
                        store(1 - q, i, q + 1)
                sp.wait_ge(xn_d, ONE + (NI - 2) * IB)
                load(0, (NI - 1) * IN_)
                store(1, 0, NI - 2)
                store(0, 0, NI - 1)
                sp.wait_ge(pad_stored, 16 * len(pads))
                for s in (xnt_stored, rows_stored):
                    for q in range(2):
                        sp.wait_ge(s[q], 16 + 16 * ((NI + 1 - q) // 2))

            @block.gpsimd
            def _(pool):
                pool.memset(k_acc[:], 0.0).then_inc(added, 1)
                pool.memset(kk_acc[:], 0.0).then_inc(added, 1)

                def back(q, t, u, ahead):
                    pool.wait_ge(kn_d, ONE + t(IB) + IB)
                    pool.wait_ge(added, ONE + t(2) + 2)
                    pool.tensor_tensor(k_acc[:], k_acc[:], k7[:], ALU.add).then_inc(added, 1)
                    pool.wait_ge(kk_d, ONE + t(IB) + IB)
                    pool.tensor_tensor(kk_acc[:], kk_acc[:], kk7[:], ALU.add).then_inc(added, 1)
                pipeline(pool, lambda q, t, u: None, back)

            @block.tensor
            def _(pe):
                pe.wait_ge(set_, ONE + 4)
                pe.matmul(ps_a[:, :], zeros[:, 0:P], zeros[:, :], start=True, stop=False, skip_group_check=True)

                def front(q, t, u):
                    for j in range(IB):
                        pe.wait_ge(xn_d, ONE + t(IB) + (j + 1))
                        pe.wait_ge(xnt_d, ONE + t(IB) + max(j - 1, 0))
                        for kh in range(2):
                            mm = pe.transpose(ps_t[j % 2][:, kh * P:(kh + 1) * P], xn7[q][:, j, kh * P:(kh + 1) * P],
                                              K.cst[:, C_ID:C_ID + P])
                        mm.then_inc(turned, 1)

                def back(q, t, u, ahead):
                    for j in range(IB):
                        pe.wait_ge(xnt_d, ONE + t(IB) + (j + 1))
                        pe.wait_ge(kb_d, ONE + t(IB) + max(j - 1, 0))
                        for kh in range(2):
                            mm = pe.matmul(ps_k[j % 2][:, 0:D], xnt7[q][:, j, kh, :], K.wk[:, kh, :],
                                           start=(kh == 0), stop=(kh == 1))
                        mm.then_inc(k_d, 1)
                        pe.wait_ge(rows_d, ONE + t(IB) + max(j - 1, 0))
                        for kh in range(2):
                            mm = pe.matmul(ps_p[j % 2][:, 0:D + 2 * HEADS], xnt7[q][:, j, kh, :], K.wcat[:, kh, :],
                                           start=(kh == 0), stop=(kh == 1))
                        mm.then_inc(proj_d, 1)
                    for j in range(IB):
                        pe.wait_ge(kn_d, ONE + t(IB) + (j + 1))
                        for kh in range(2):
                            mm = pe.matmul(ps_a[:, kh * D:(kh + 1) * D], xn7[q][:, j, kh * P:(kh + 1) * P], k7[:, j, :],
                                           start=False, stop=False, skip_group_check=True)
                        mm.then_inc(sums_d, 1)
                    if ahead:
                        front(*ahead)
                pipeline(pe, front, back)
                pe.wait_ge(col_d, ONE + 2)
                for k in range(2):
                    for kh in range(2):
                        pe.matmul(ps_s[:, 2 * k + kh:2 * k + kh + 1], col[:, k, kh * P:(kh + 1) * P], ones[:, 0:1],
                                  start=True, stop=True).then_inc(col_mm, 1)
                pe.wait_ge(fin, ONE + 2)
                for mh in range(2):
                    for kh in range(2):
                        pe.matmul(ps_p[mh][:, 0:D], att[:, kh, mh * P:(mh + 1) * P], K.wvo[:, kh, :],
                                  start=(kh == 0), stop=(kh == 1)).then_inc(end_mm, 1)

            @block.scalar
            def _(act):
                def front(q, t, u):
                    act.wait_ge(var_d, ONE + t(1) + 1)
                    act.activation(var[:, 1, :], var[:, 0, :], ACT.Sqrt).then_inc(std_d, 1)

                def back(q, t, u, ahead):
                    for j in range(IB):
                        act.wait_ge(kb_d, ONE + t(IB) + (j + 1))
                        act.activation(k7[:, j, :], k7[:, j, :], ACT.Square, accum_out=ks7[:, 0, j:j + 1]).then_inc(k2_d, 1)
                        if j == 0:
                            act.wait_ge(rows_stored[q], u(16) + 16)
                            act.wait_ge(init_d, ONE + t(2))
                        act.wait_ge(proj_d, ONE + t(IB) + (j + 1))
                        act.copy(rows7[q][:, j, 0:RW].rearrange("p (h c) -> p h c", c=HC)[:, :, 0:HD],
                                 ps_p[j % 2][:, 0:D].rearrange("p (h c) -> p h c", c=HD))
                        act.copy(rows7[q][:, j, RW:RW + 2 * HEADS], ps_p[j % 2][:, D:D + 2 * HEADS]).then_inc(rows_d, 1)
                    act.wait_ge(rows_d, ONE + t(IB) + IB)
                    act.dma_start(dr["table"][bass.ds(t(IN_), IN_), :].rearrange("(j p) c -> p j c", p=P),
                                  rows7[q][:, :, 0:TW]).then_inc(rows_stored[q], 16)
                    act.wait_ge(added, ONE + t(2) + 2)
                    for j in range(IB):
                        act.wait_ge(kn_d, ONE + t(IB) + (j + 1))
                        act.activation(kk7[:, j, :], k7[:, j, :], ACT.Square).then_inc(kk_d, 1)
                        if j == 0 and ahead:
                            front(*ahead)
                pipeline(act, front, back)
                act.wait_ge(fin, ONE + 2)
                act.activation(ssb[:, 4:6], ssb[:, 2:4], ACT.Sqrt).then_inc(end_sq, 1)

            @block.vector
            def _(dve):
                dve.memset(ones[:], 1.0).then_inc(set_, 1)
                dve.memset(zeros[:], 0.0).then_inc(set_, 1)
                for q in range(2):
                    dve.memset(rows7[q][:], 1.0).then_inc(set_, 1)

                def stat(j, q, t, u):
                    if j == 0:
                        dve.wait_ge(x_in[q], u(16) + 16)
                    dve.bn_stats(stats[:, j, :], x7[q][:, j, :]).then_inc(stats_d, 1)

                def variance(q, t, u):
                    dve.wait_ge(stats_d, ONE + t(IB) + IB)
                    settle(dve, settled)
                    for j in range(IB):
                        dve.bn_aggr(mv[:, j, :], stats[:, j, :]).then_inc(aggr_d, 1)
                    dve.wait_ge(aggr_d, ONE + t(IB) + IB)
                    dve.tensor_scalar(var[:, 0, :].unsqueeze(2), mv[:, :, 1:2], LN_EPS, None, ALU.add).then_inc(var_d, 1)

                def norm(q, t, u):
                    dve.wait_ge(std_d, ONE + t(1) + 1)
                    dve.reciprocal(var[:, 1, :], var[:, 1, :]).then_inc(rstd_d, 1)
                    dve.wait_ge(rstd_d, ONE + t(1) + 1)
                    for j in range(IB):
                        dve.tensor_scalar(xn7[q][:, j, :], x7[q][:, j, :], mv[:, j, 0:1], var[:, 1, j:j + 1],
                                          ALU.subtract, ALU.mult).then_inc(xn_d, 1)

                def turn(q, t, u):
                    dve.wait_ge(xnt_stored[q], u(16) + 16)
                    for j in range(IB):
                        dve.wait_ge(turned, ONE + t(IB) + (j + 1))
                        dve.tensor_copy(xnt7[q][:, j, :, :].rearrange("p k n -> p (k n)"), ps_t[j % 2][:, 0:2 * P]).then_inc(xnt_d, 1)

                def front(q, t, u):
                    for j in range(IB):
                        stat(j, q, t, u)
                    variance(q, t, u)
                    norm(q, t, u)
                    turn(q, t, u)

                def back(q, t, u, ahead):
                    dve.wait_ge(sums_d, ONE + t(IB))
                    dve.wait_ge(kk_d, ONE + t(IB))
                    dve.wait_ge(added, ONE + t(2) + 1)
                    for j in range(IB):
                        dve.wait_ge(k_d, ONE + t(IB) + (j + 1))
                        dve.tensor_tensor(k7[:, j, :], ps_k[j % 2][:, 0:D], K.bk[:], ALU.add).then_inc(kb_d, 1)
                        if ahead:
                            stat(j, *ahead)
                    if ahead:
                        variance(*ahead)
                    dve.wait_ge(k2_d, ONE + t(IB) + IB)
                    dve.tensor_scalar(ks7[:, 1, :], ks7[:, 0, :], DIV_EPS, None, ALU.add).then_inc(r1_d, 1)
                    dve.wait_ge(r1_d, ONE + t(1) + 1)
                    dve.reciprocal(ks7[:, 2, :], ks7[:, 1, :]).then_inc(r2_d, 1)
                    dve.wait_ge(r2_d, ONE + t(1) + 1)
                    dve.tensor_tensor(ks7[:, 1, :], ks7[:, 2, :], K.cst[:, bass.ds(t(IB) + C_VALID, IB)], ALU.mult).then_inc(r3_d, 1)
                    dve.wait_ge(r3_d, ONE + t(1) + 1)
                    for j in range(IB):
                        dve.tensor_scalar(k7[:, j, :], k7[:, j, :], ks7[:, 1, j:j + 1], None, ALU.mult).then_inc(kn_d, 1)
                    if ahead:
                        norm(*ahead)
                    dve.wait_ge(rows_d, ONE + t(IB) + IB)
                    settle(dve, settled)
                    at = bass.ds(t(IB), IB)
                    dve.tensor_copy(K.acc[:, at, :], rows7[q][:, :, 0:RW]).then_inc(init_d, 1)
                    dve.tensor_copy(K.state[:, at, :], rows7[q][:, :, RW:RW + 2 * HEADS]).then_inc(init_d, 1)
                    if ahead:
                        turn(*ahead)
                pipeline(dve, front, back)
                link = chain(dve, dch)
                dve.wait_ge(added, ONE + 2 * NI + 2)
                for k, a in enumerate((k_acc, kk_acc)):
                    dve.tensor_reduce(col[:, k, :], a[:].rearrange("p j c -> p c j"), AX, ALU.add).then_inc(col_d, 1)
                dve.wait_ge(sums_d, ONE + NI * IB)
                dve.tensor_copy(att[:], ps_a[:].rearrange("p (a b) -> p a b", b=D)).then_inc(fin, 1)
                dve.wait_ge(col_mm, ONE + 4)
                dve.tensor_copy(ssb[:, 0:4], ps_s[:, 0:4]).then_inc(fin, 1)
                link(dve.memset(K.kvw[:, :, D:D + 1], 1.0))
                dve.wait_ge(end_sq, ONE + 1)
                link(dve.tensor_scalar(ssb[:, 6:8], ssb[:, 4:6], NORM_EPS, float(N) ** 0.5, ALU.max, ALU.mult))
                link(dve.reciprocal(ssb[:, 6:8], ssb[:, 6:8]))
                dve.wait_ge(end_mm, ONE + 4)
                for mh in range(2):
                    link(dve.scalar_tensor_tensor(K.kvw[:, mh, 0:D], K.bvw[:], ssb[:, mh:mh + 1], ps_p[mh][:, 0:D],
                                                  ALU.mult, ALU.add))
                    link(dve.tensor_scalar(K.kvw[:, mh, 0:D], K.kvw[:, mh, 0:D], ssb[:, 6 + mh:7 + mh], None, ALU.mult))


def attend(nc, dr, K):
    with ExitStack() as ctx:
        m = Mem(nc, ctx)
        xg = [m.sb(f"xg{q}", [P, SV, CH, TW]) for q in range(2)]
        idx = [m.sb(f"idx{q}", [P, SV * CH], I32) for q in range(2)]
        hot = [m.sb(f"hot{q}", [P, SV, CH, P], BF16) for q in range(2)]
        hotw = [m.sb(f"hotw{q}", [P, CH, P]) for q in range(2)]
        hot_t = m.sb("hot_t", [P, SV, CH * P], BF16)
        y = [m.sb(f"y{q}", [P, CH, RW]) for q in range(2)]
        dlist = [m.sb(f"dlist{q}", [HEADS * SV, GE], I32) for q in range(2)]
        dbig = m.sb("dbig", [HEADS * SV, GE])
        step_ = m.sb("seg_step", [HEADS * SV, GE])
        asrc = m.sb("asrc", [P, CH, HEADS, SV])
        fmax = m.sb("fmax", [HEADS * SV, GE])
        tails = m.sb("tails", [P, 2, SV, CH, HEADS])
        tail = m.sb("tail", [P, SV, CH, 3 * HEADS + 1], BF16)
        pair_rest = m.sb("pair_rest", [P, 2, HEADS * SV])
        pair = m.sb("pair", [P, 3, 2 * HEADS, SV], BF16)
        st = m.sb("st", [P, 4 + 3 * HEADS * SV])
        sv_ = m.sb("sv", [P, HEADS * SV])
        gone = m.sb("gone", [P, SV])
        zz = m.sb("zz", [P, 4, HEADS * SV])
        fo = m.sb("fo", [P, HEADS * SV])
        sc = m.sb("sc", [P, SV * CH * HEADS])
        w = m.sb("w", [P, SV * CH, HEADS])
        ps_t, ps_fm, ps_l, ps_q = (m.ps(n, [P, 512]) for n in ("ps_at", "ps_fm", "ps_l", "ps_q"))
        NM = 3 * HEADS + 1
        ps_f, ps_m = ps_fm[:, 0:CH * HEADS * SV], ps_fm[:, CH * HEADS * SV:CH * HEADS * SV + SV * NM]
        xb = m.sb("xb", [P, 2, P])
        q2t, q4t = m.sb("q2t", [P, 2, P]), m.sb("q4t", [P, 2, P])
        mixed = m.sb("mixed", [P, MW])
        xb_in, mix_out = m.sem("xb_in"), m.sem("mix_out")
        ps_o = [m.ps(f"ps_o{i}", [P, 2 * CH * P], BF16) for i in range(2)]
        ps_y = [m.ps(f"ps_y{i}", [P, 512]) for i in range(2)]
        got = [[m.sem(f"gathered{q}_{v}") for v in range(SV)] for q in range(2)]
        settled = m.count("settled_a")
        dl_in = [m.sem(f"dlist_in{q}") for q in range(2)]
        (idx_d, hot_d, dbig_d, step_d, at_d, fmax_d, ft_d, tail_d, sm_d, loaded, gone_d, sv_d, mx_d, run_d,
         saved, old1, old_d, z_d, lk_d, fa_d, fo_d, ho_d, ht_d, look_d, s1_d, s2_d, s3_d, s4_d, w_d,
         vo_d, qt_d, q2_d, q4_d, mix_d, mixc_d, hotw_d, ya_d, msum_d, tp1_d, tp2_d, tp3_d, pp_d, z1_d, lk1_d,
         y_d, py_d, sc_d, acc_d, as_d) = map(m.count, (
            "idx_staged", "hot_built", "dst_scaled", "segments_done", "asrc_turned", "fmax_done", "fmax_turned",
            "tails_done", "max_summed", "state_loaded", "gone_done", "sv_done", "max_with_state", "running_max",
            "state_saved", "old_shifted", "old_done", "fold_z", "fold_leaky", "fold_arg", "fold_done", "hot_turned",
            "hot_t_done", "looked_up", "score_z", "score_leaky", "score_less", "score_capped",
            "weights_done", "values_copied", "q_turned", "q_squared", "q_fourth", "mix_products", "mix_copied", "hot_widened", "y_done_act", "max_joined", "tail_first", "tail_second", "tail_third",
            "pair_parts", "max_shifted", "max_leaky", "y_done", "y_summed", "acc_scaled", "acc_done", "asrc_packed"))
        YV = CH - 1
        SN, S0, S1, S2 = 1, 1, 1 + HEADS * SV, 1 + 2 * HEADS * SV

        def hv(t, at):
            return t[:, at:at + HEADS * SV].rearrange("p (h v) -> p h v", v=SV)

        def steps(eng, body):
            with eng.Fori(0, NS // 2) as i:
                for q in range(2):
                    body(q, i, lambda k, q=q, i=i: i * (2 * k) + q * k)
            if NS % 2:
                body(0, NS // 2, lambda k: (NS - 1) * k)

        m.start_counts(((mix_out, 16), (y_d, 2 * SV), (ya_d, 2 * SV), (dbig_d, 1)))
        with nc.Block() as block:
            @block.gpsimd
            def _(pool):
                def body(q, i, n):
                    pool.wait_ge(idx_d, ONE + n(1) + 1)
                    for v in range(SV):
                        pool.wait_ge(y_d, ONE + n(SV) + (v + 1))
                        pool.wait_ge(ya_d, ONE + n(SV) + (v + 1))
                        settle(pool, settled)
                        for j in range(CH):
                            c = v * CH + j
                            pool.indirect_dma_start(
                                xg[q][:, v, j, :], None, dr["table"],
                                bass.IndirectOffsetOnAxis(ap=idx[q][:, c:c + 1], axis=0)).then_inc(got[q][v], 16)
                steps(pool, body)

            @block.sync
            def _(sp):
                def body(q, i, n):
                    sp.wait_ge(qt_d, ONE + n(1))
                    settle(sp, settled)
                    sp.dma_start(xb[:].rearrange("p k n -> p (k n)"),
                                 dr["xnt"][bass.ds(n(1), 1)].rearrange("o p c -> (o p) c")).then_inc(xb_in, 16)
                    sp.wait_ge(dbig_d, ONE + n(1))
                    for h in range(HEADS):
                        sp.dma_start(dlist[q][h * SV:(h + 1) * SV, :],
                                     dr["dst"][bass.ds(n(SV), SV), :]).then_inc(dl_in[q], 16)
                    sp.wait_ge(mixc_d, ONE + n(1) + 1)
                    settle(sp, settled)
                    sp.dma_start(dr["mix"][bass.ds(n(P), P), :], mixed[:]).then_inc(mix_out, 16)
                steps(sp, body)
                sp.wait_ge(mix_out, 16 + 16 * NS)

            @block.scalar
            def _(act):
                def body(q, i, n):
                    act.wait_ge(dl_in[q], i * (16 * HEADS) + 16 * HEADS)
                    act.wait_ge(step_d, ONE + n(2))
                    act.mul(dbig[:], dlist[q][:], BIG).then_inc(dbig_d, 1)
                    for v in range(SV):
                        act.wait_ge(got[q][v], i * (16 * CH) + 16 * CH)
                    act.wait_ge(at_d, ONE + n(CH))
                    act.copy(asrc[:], xg[q][:, :, :, RW:TW].rearrange("p v j h -> p j h v")).then_inc(as_d, 1)
                    act.wait_ge(look_d, ONE + n(1))
                    for p in range(SV // 2):
                        act.wait_ge(ho_d, ONE + n(SV // 2) + (p + 1))
                        act.copy(hot_t[:, 2 * p:2 * p + 2, :].rearrange("p v n -> p (v n)"), ps_o[p % 2][:]).then_inc(ht_d, 1)
                    act.wait_ge(qt_d, ONE + n(1) + 1)
                    act.wait_ge(mix_d, ONE + n(1))
                    act.wait_ge(mix_out, n(16) + 16)
                    for mh in range(2):
                        act.activation(q2t[:, mh, :], ps_q[:, mh * P:(mh + 1) * P], ACT.Square,
                                       bias=K.bqc[:, mh:mh + 1]).then_inc(q2_d, 1)
                    act.wait_ge(q2_d, ONE + n(2) + 2)
                    act.activation(q4t[:], q2t[:], ACT.Square).then_inc(q4_d, 1)
                    act.copy(mixed[:, D + 2:MW], ps_q[:, D:2 * D]).then_inc(vo_d, 1)
                    for v in range(2):
                        widen(v, q, n)
                    act.wait_ge(mix_d, ONE + n(1) + 1)
                    act.copy(mixed[:, 0:D + 2], ps_q[:, 0:D + 2]).then_inc(mixc_d, 1)
                    act.wait_ge(fa_d, ONE + n(1) + 1)
                    act.wait_ge(acc_d, ONE + n(SV))
                    act.activation(fo[:], zz[:, 3, :], ACT.Exp).then_inc(fo_d, 1)
                    act.wait_ge(s4_d, ONE + n(1) + 1)
                    act.activation(w[:], sc[:].rearrange("p (c h) -> p c h", h=HEADS), ACT.Exp).then_inc(w_d, 1)
                    for v in range(SV):
                        if v >= 2:
                            widen(v, q, n)
                        act.wait_ge(w_d, ONE + n(1) + 1)
                        act.wait_ge(py_d, ONE + n(SV) + max(v - 1, 0))
                        for h in range(HEADS):
                            at = slice(h * HC, (h + 1) * HC)
                            mul = act.activation(y[v % 2][:, YV, at], xg[q][:, v, YV, at], ACT.Copy,
                                                 scale=w[:, v * CH + YV, h:h + 1])
                        mul.then_inc(ya_d, 1)

                def widen(v, q, n):
                    act.wait_ge(hot_d, ONE + n(4) + 4)
                    act.wait_ge(py_d, ONE + n(SV) + max(v - 1, 0))
                    act.copy(hotw[v % 2][:], hot[q][:, v, :, :]).then_inc(hotw_d, 1)
                steps(act, body)

            @block.tensor
            def _(pe):
                ident = K.cst[:, C_ID:C_ID + P]

                def body(q, i, n):
                    pe.wait_ge(fmax_d, ONE + n(1))
                    pe.wait_ge(as_d, ONE + n(1) + 1)
                    for j in range(CH):
                        pe.transpose(ps_t[0:HEADS * SV, j * P:(j + 1) * P],
                                     asrc[:, j, :, :].rearrange("p h v -> p (h v)"), ident).then_inc(at_d, 1)
                    pe.wait_ge(hot_d, ONE + n(4) + 4)
                    for v in range(SV):
                        p = v // 2
                        pe.wait_ge(ht_d, ONE + n(SV // 2) + max(p - 1, 0))
                        for j in range(CH):
                            at = (v % 2 * CH + j) * P
                            mm = pe.transpose(ps_o[p % 2][:, at:at + P], hot[q][:, v, j, :], K.cstb[:, 0:P])
                        if v % 2:
                            mm.then_inc(ho_d, 1)
                    pe.wait_ge(fmax_d, ONE + n(1) + 1)
                    pe.wait_ge(tail_d, ONE + n(2))
                    settle(pe, settled)
                    for j in range(CH):
                        pe.transpose(ps_f[:, j * HEADS * SV:(j + 1) * HEADS * SV], fmax[:, j * P:(j + 1) * P],
                                     ident[0:HEADS * SV, 0:HEADS * SV]).then_inc(ft_d, 1)
                    pe.wait_ge(xb_in, n(16) + 16)
                    pe.wait_ge(mixc_d, ONE + n(1))
                    for mh in range(2):
                        for kh in range(2):
                            mm = pe.matmul(ps_q[:, mh * P:(mh + 1) * P], K.wq[:, kh, mh * P:(mh + 1) * P], xb[:, kh, :],
                                           start=(kh == 0), stop=(kh == 1))
                    for kh in range(2):
                        mm = pe.matmul(ps_q[:, D:2 * D], xb[:, kh, :], K.wvo[:, kh, :], start=(kh == 0), stop=(kh == 1))
                    mm.then_inc(qt_d, 1)
                    pe.wait_ge(tp3_d, ONE + n(1) + 1)
                    pe.wait_ge(sv_d, ONE + n(1))
                    for v in range(SV):
                        for j in range(CH):
                            mm = pe.matmul(ps_m[:, v * NM:(v + 1) * NM], hot[q][:, v, j, :], tail[:, v, j, :],
                                           start=(j == 0), stop=(j == CH - 1))
                    mm.then_inc(sm_d, 1)
                    pe.wait_ge(q4_d, ONE + n(1) + 1)
                    pe.wait_ge(vo_d, ONE + n(1) + 1)
                    for kh in range(2):
                        pe.matmul(ps_q[:, 0:D + 1], q2t[:, kh, :], K.kvw[:, kh, :], start=(kh == 0), stop=(kh == 1))
                    for kh in range(2):
                        mm = pe.matmul(ps_q[:, D + 1:D + 2], q4t[:, kh, :], K.kvw[:, kh, D:D + 1], start=(kh == 0), stop=(kh == 1))
                    mm.then_inc(mix_d, 1)
                    pe.wait_ge(ht_d, ONE + n(SV // 2) + SV // 2)
                    pe.wait_ge(pp_d, ONE + n(8) + 8)
                    pe.wait_ge(s3_d, ONE + n(1))
                    for v in range(SV):
                        for j in range(CH):
                            c = v * CH + j
                            for k in range(3):
                                mm = pe.matmul(ps_l[:, c * 8:c * 8 + 8], hot_t[:, v, j * P:(j + 1) * P], pair[:, k, :, v],
                                               start=(k == 0), stop=(k == 2))
                    mm.then_inc(look_d, 1)
                    for v in range(SV):
                        pe.wait_ge(hotw_d, ONE + n(SV) + (v + 1))
                        pe.wait_ge(y_d, ONE + n(SV) + (2 * SV + v + 1))
                        pe.wait_ge(acc_d, ONE + n(SV) + max(v - 1, 0))
                        for j in range(CH):
                            if j == YV:
                                pe.wait_ge(ya_d, ONE + n(SV) + (2 * SV + v + 1))
                            mm = pe.matmul(ps_y[v % 2][:, 0:RW], hotw[v % 2][:, j, :], y[v % 2][:, j, :],
                                           start=(j == 0), stop=(j == CH - 1))
                        mm.then_inc(py_d, 1)
                steps(pe, body)

            @block.vector
            def _(dve):
                dve.memset(st[:], 0.0).then_inc(gone_d, 1)
                dve.wait_ge(gone_d, ONE + 1)
                flat = HEADS * SV

                def build(part, q, at):
                    k = SV // 4
                    rel = K.rel[:, bass.ds(at + part * (k * CH), k * CH)]
                    dve.tensor_tensor(hot[q][:, part * k:(part + 1) * k, :, :].rearrange("p v j n -> p (v j) n"),
                                      bc(K.cstb[:, P:2 * P], 1, k * CH), bc(rel, 2, P), ALU.is_equal).then_inc(hot_d, 1)
                for q in range(2):
                    dve.tensor_copy(idx[q][:], K.ix[:, q * SV * CH:(q + 1) * SV * CH]).then_inc(idx_d, 1)
                for part in range(4):
                    build(part, 0, 0)

                def body(q, i, n):
                    nxt = 1 - q, n(SV * CH) + SV * CH
                    dve.wait_ge(dbig_d, ONE + n(1) + 2)
                    dve.memset(step_[:, 0:1], 0.0).then_inc(step_d, 1)
                    dve.tensor_tensor(step_[:, 1:GE], dbig[:, 0:GE - 1], dbig[:, 1:GE], ALU.subtract).then_inc(step_d, 1)
                    dve.wait_ge(step_d, ONE + n(2) + 2)
                    dve.wait_ge(at_d, ONE + n(CH) + CH)
                    dve.tensor_tensor_scan(fmax[:], step_[:], ps_t[0:flat, :], -BIG, ALU.add, ALU.max).then_inc(fmax_d, 1)
                    words = [dve.value_load(K.blk[0:1, bass.ds(n(2) + k, 1)], min_val=0, max_val=(1 << 24) - 1)
                             for k in range(2)]
                    blk = [nc.s_assert_within(dve.snap((words[v // 4] >> (6 * (v % 4))) & 63), 0, NB - 1, skip_runtime_bounds_check_because="destinations are nodes")
                           for v in range(SV)]
                    last = K.last[:, bass.ds(n(SV * CH), SV * CH)].rearrange("p (v j) -> p v j", j=CH)
                    dve.wait_ge(ft_d, ONE + n(CH) + CH)
                    dve.wait_ge(sm_d, ONE + n(1))
                    kept = ps_f[:, 0:CH * flat].rearrange("p (j h v) -> p h v j", h=HEADS, v=SV)
                    parts = [tail[:, :, :, k * HEADS:(k + 1) * HEADS] for k in range(3)]
                    dve.tensor_tensor(parts[0].rearrange("p v j h -> p h v j"), kept, bc(last, 1, HEADS), ALU.mult).then_inc(tp1_d, 1)
                    dve.tensor_tensor(tails[:, 0].rearrange("p v j h -> p h v j"), kept, bc(last, 1, HEADS), ALU.mult).then_inc(tail_d, 1)
                    dve.tensor_copy(tail[:, :, :, 3 * HEADS], last).then_inc(tail_d, 1)
                    dve.wait_ge(tp1_d, ONE + n(1) + 1)
                    dve.wait_ge(tail_d, ONE + n(2) + 2)
                    dve.tensor_tensor(tails[:, 1], tails[:, 0], parts[0], ALU.subtract).then_inc(msum_d, 1)
                    dve.wait_ge(msum_d, ONE + n(2) + 1)
                    dve.tensor_copy(parts[1], tails[:, 1]).then_inc(tp2_d, 1)
                    dve.wait_ge(tp2_d, ONE + n(1) + 1)
                    dve.tensor_tensor(parts[2], tails[:, 1], parts[1], ALU.subtract).then_inc(tp3_d, 1)
                    dve.wait_ge(saved, ONE + n(SV))
                    dve.wait_ge(look_d, ONE + n(1))
                    dve.wait_ge(hotw_d, ONE + n(SV))
                    settle(dve, settled)
                    if not isinstance(i, int):
                        dve.tensor_copy(idx[q][:], K.ix[:, bass.ds(n(SV * CH) + 2 * SV * CH, SV * CH)]).then_inc(idx_d, 1)
                    build(1, *nxt)
                    for v in range(SV):
                        dve.tensor_copy(st[:, S1:S1 + 2 * flat].rearrange("p (s v) -> p s v", v=SV)[:, :, v:v + 1],
                                        K.state[:, bass.ds(blk[v], 1), :].rearrange("p o s -> p s o")).then_inc(loaded, 1)
                    dve.wait_ge(loaded, ONE + n(SV) + SV)
                    for _ in split(1, st[:, S2:S2 + flat], n):
                        pass
                    dve.wait_ge(sm_d, ONE + n(1) + 1)
                    pm = ps_m[:, 0:SV * NM].rearrange("p (v s) -> p v s", s=NM)
                    dve.tensor_reduce(zz[:, 2, :].rearrange("p (h v) -> p h v", v=SV),
                                      pm[:, :, 0:3 * HEADS].rearrange("p v (k h) -> p h v k", h=HEADS), AX, ALU.add).then_inc(msum_d, 1)
                    dve.tensor_scalar(gone[:].unsqueeze(2), pm[:, :, NM - 1:NM], -1.0, BIG, ALU.add, ALU.mult).then_inc(gone_d, 1)
                    dve.wait_ge(gone_d, ONE + n(1) + 2)
                    dve.wait_ge(msum_d, ONE + n(2) + 2)
                    dve.tensor_tensor(sv_[:].rearrange("p (h v) -> p h v", v=SV), hv(zz[:, 2, :], 0),
                                      bc(gone[:], 1, HEADS), ALU.add).then_inc(sv_d, 1)
                    dve.wait_ge(sv_d, ONE + n(1) + 1)
                    dve.tensor_tensor(sv_[:], sv_[:], st[:, S1:S1 + flat], ALU.max).then_inc(mx_d, 1)
                    dve.wait_ge(mx_d, ONE + n(1) + 1)
                    brk = K.brk[:, bass.ds(n(1), 1), :, :].rearrange("p o h v -> p (o h v)")
                    dve.tensor_tensor_scan(st[:, SN:SN + flat], brk, sv_[:], -BIG, ALU.add, ALU.max).then_inc(run_d, 1)
                    dve.wait_ge(run_d, ONE + n(1) + 1)
                    def save(v):
                        dve.wait_ge(saved, ONE + n(SV) + v)
                        dve.tensor_scalar(K.state[:, bass.ds(blk[v], 1), 0:HEADS].rearrange("p o s -> p s o"),
                                          hv(st, SN)[:, :, v:v + 1], 1.0, None, ALU.mult).then_inc(saved, 1)
                    dve.tensor_tensor(zz[:, 1, :], st[:, SN:SN + flat], st[:, S2:S2 + flat], ALU.add).then_inc(z1_d, 1)
                    dve.tensor_tensor(zz[:, 0, :], st[:, SN - 1:SN - 1 + flat], brk, ALU.add).then_inc(old1, 1)
                    dve.wait_ge(z1_d, ONE + n(1) + 1)
                    dve.scalar_tensor_tensor(zz[:, 1, :], zz[:, 1, :], SLOPE, zz[:, 1, :], ALU.mult, ALU.max).then_inc(lk1_d, 1)
                    dve.wait_ge(old1, ONE + n(1) + 1)
                    dve.tensor_tensor(zz[:, 0, :], zz[:, 0, :], st[:, S1:S1 + flat], ALU.max).then_inc(old_d, 1)
                    dve.wait_ge(lk1_d, ONE + n(1) + 1)
                    link = split(0, zz[:, 1, :], n)
                    next(link)
                    dve.wait_ge(old_d, ONE + n(1) + 1)
                    dve.tensor_tensor(zz[:, 0, :], zz[:, 0, :], st[:, S2:S2 + flat], ALU.add).then_inc(z_d, 1)
                    next(link)
                    dve.wait_ge(z_d, ONE + n(1) + 1)
                    dve.scalar_tensor_tensor(zz[:, 0, :], zz[:, 0, :], SLOPE, zz[:, 0, :], ALU.mult, ALU.max).then_inc(lk_d, 1)
                    next(link)
                    dve.wait_ge(lk_d, ONE + n(1) + 1)
                    dve.wait_ge(fo_d, ONE + n(1))
                    dve.tensor_tensor(zz[:, 3, :], zz[:, 0, :], zz[:, 1, :], ALU.subtract).then_inc(fa_d, 1)
                    next(link)
                    for v in range(SV):
                        save(v)
                    build(2, *nxt)
                    dve.wait_ge(look_d, ONE + n(1) + 1)
                    lk = ps_l[:, 0:SV * CH * 2 * HEADS].rearrange("p (v j s) -> p v j s", j=CH, s=2 * HEADS)
                    scv = sc[:].rearrange("p (v j h) -> p v j h", j=CH, h=HEADS)
                    dve.wait_ge(w_d, ONE + n(1))
                    dve.tensor_tensor(scv, xg[q][:, :, :, RW:TW], lk[:, :, :, HEADS:2 * HEADS], ALU.add).then_inc(s1_d, 1)
                    dve.wait_ge(s1_d, ONE + n(1) + 1)
                    dve.scalar_tensor_tensor(sc[:], sc[:], SLOPE, sc[:], ALU.mult, ALU.max).then_inc(s2_d, 1)
                    dve.wait_ge(s2_d, ONE + n(1) + 1)
                    dve.tensor_tensor(scv, scv, lk[:, :, :, 0:HEADS], ALU.subtract).then_inc(s3_d, 1)
                    dve.wait_ge(s3_d, ONE + n(1) + 1)
                    dve.tensor_scalar(sc[:], sc[:], 0.0, None, ALU.min).then_inc(s4_d, 1)
                    dve.wait_ge(w_d, ONE + n(1) + 1)
                    dve.wait_ge(fo_d, ONE + n(1) + 1)
                    for v in range(SV + 1):
                        if v < SV:
                            dve.wait_ge(py_d, ONE + n(SV) + max(v - 1, 0))
                            dve.tensor_tensor(y[v % 2][:, 0:YV].rearrange("p j (h c) -> p j h c", c=HC),
                                              xg[q][:, v, 0:YV, 0:RW].rearrange("p j (h c) -> p j h c", c=HC),
                                              bc(w[:, v * CH:v * CH + YV, :], 3, HC), ALU.mult).then_inc(y_d, 1)
                        if v == 1:
                            build(3, *nxt)
                            build(0, *nxt)
                        if v > 0:
                            scale(v - 1, blk[v - 1], n)
                            add_up(v - 1, blk[v - 1], n)

                def split(k, src, n):
                    part = [pair[:, t, k * HEADS:(k + 1) * HEADS, :].rearrange("p h v -> p (h v)") for t in range(3)]
                    rest, done = pair_rest[:, k, :], 8 if k == 0 else 4
                    yield dve.tensor_copy(part[0], src).then_inc(pp_d, 1)
                    dve.wait_ge(pp_d, ONE + n(8) + (done - 3))
                    yield dve.tensor_tensor(rest, src, part[0], ALU.subtract).then_inc(pp_d, 1)
                    dve.wait_ge(pp_d, ONE + n(8) + (done - 2))
                    yield dve.tensor_copy(part[1], rest).then_inc(pp_d, 1)
                    dve.wait_ge(pp_d, ONE + n(8) + (done - 1))
                    yield dve.tensor_tensor(part[2], rest, part[1], ALU.subtract).then_inc(pp_d, 1)

                def sums(blk):
                    return K.acc[:, bass.ds(blk, 1), :].rearrange("p o (h c) -> p (o h) c", c=HC)

                def scale(v, blk, n):
                    dve.wait_ge(acc_d, ONE + n(SV) + v)
                    dve.tensor_tensor(sums(blk), sums(blk), bc(hv(fo, 0)[:, :, v], 2, HC), ALU.mult).then_inc(sc_d, 1)

                def add_up(v, blk, n):
                    dve.wait_ge(sc_d, ONE + n(SV) + (v + 1))
                    dve.wait_ge(py_d, ONE + n(SV) + (v + 1))
                    dve.tensor_tensor(sums(blk), sums(blk), ps_y[v % 2][:, 0:RW].rearrange("p (h c) -> p h c", c=HC), ALU.add).then_inc(acc_d, 1)
                steps(dve, body)


def experts(nc, io, dr, K):
    with ExitStack() as ctx:
        m = Mem(nc, ctx)
        w1 = m.sb("w1", [P, 2, E, D])
        w2 = m.sb("w2", [P, 2, E, D])
        wo = m.sb("wo", [P, 2, E, D])
        h1 = m.sb("h1", [P, 2, IN_])
        h2 = m.sb("h2", [P, 2, IN_])
        zt = [m.sb(f"zt{q}", [P, 2, IN_]) for q in range(2)]
        yb = [m.sb(f"yb{q}", [P, IB, D]) for q in range(2)]
        x7 = m.sb("x7e", [P, IB, D])
        q7 = m.sb("q7", [P, IB, D])
        t7 = m.sb("t7", [P, IB, MW])
        bo = m.sb("bo", [P, E, D])
        wts = [m.sb(f"wts{q}", [P, IB, E]) for q in range(2)]
        lg = m.sb("lg", [P, IB, E])
        small = m.sb("small", [P, 10, IB])
        den = m.sb("den", [P, IB, HEADS])
        stats = m.sb("stats_e", [P, IB, 6])
        mv = m.sb("mv_e", [P, IB, 2])
        ps_h = [m.ps(f"ps_h{i}", [P, 512]) for i in range(4)]
        ps_y = [m.ps(f"ps_ye{i}", [P, 512]) for i in range(2)]
        ps_n = [m.ps(f"ps_n{i}", [P, 512]) for i in range(2)]
        w_in = [m.sem(f"experts_in{e}") for e in range(E)]
        bo_in, x_in, mix_in, out_d = m.sem("bo_in"), m.sem("x_in_e"), m.sem("mix_in"), m.sem("out_stored")
        names = """node_products node_reads hidden_products hidden_done expert_products expert_added
            q_small1 q_small2 q_root q_small3 q_small4 q_small5 q_small6
            mix_scaled z_based z_const den_done gat_done z_done stats_done_e aggr_done_e var_done_e std_done_e
            rstd_done_e zn_done zt_done lg_done lg_max lg_less lg_exp lg_sum lg_rec wts_done biased settled_e stored"""
        S = {k: m.count("s_" + k) for k in names.split()}
        HALF = (IB + 1) // 2
        NPR = 2 * IB
        HB = 8

        def stages(eng, node, expert):
            for k in range(5):
                node(k, 0, lambda c: 0, None)

            def iteration(q, t, more):
                for e in range(E):
                    expert(e, q, t)
                    if more and e < 5:
                        node(e, 1 - q, lambda c: t(c) + c, t)
                    if e in (5, 6):
                        node(e, q, t, None)
            with eng.Fori(0, NI // 2) as i:
                for q in range(2):
                    iteration(q, lambda c, q=q, i=i: i * (2 * c) + q * c, True)
            iteration(0, lambda c: (NI - 1) * c, False)

        m.start_counts(((S["hidden_done"], 4),))
        with nc.Block() as block:
            @block.sync
            def _(sp):
                def node(k, q, t, before):
                    if k == 0:
                        if before:
                            sp.wait_ge(S["z_done"], ONE + t(IB))
                            settle(sp, S["settled_e"])
                            sp.wait_ge(S["node_products"], ONE + t(NPR))
                            settle(sp, S["settled_e"])
                        sp.dma_start(t7[:], dr["mix"][bass.ds(t(IN_), IN_), :].rearrange("(j p) c -> p j c", p=P)).then_inc(mix_in, 16)
                        sp.dma_start(x7[:], io["x"][bass.ds(t(IN_), IN_), :].rearrange("(j p) c -> p j c", p=P)).then_inc(x_in, 16)
                        if not before:
                            sp.dma_start(bo[:].rearrange("p e d -> p (e d)"),
                                         io["b_o"].rearrange("e d -> (e d)").partition_broadcast(P)).then_inc(bo_in, 16)
                            for e in range(E):
                                for dst, name in ((w1, "w1"), (w2, "w2"), (wo, "wo")):
                                    sp.dma_start(dst[:, :, e, :], io[name][:, :, e, :]).then_inc(w_in[e], 16)

                def expert(e, q, t):
                    if e == E - 1:
                        sp.wait_ge(S["expert_added"], ONE + t(E * IB) + E * IB)
                        sp.dma_start(io["out"][bass.ds(t(IN_), IN_), :].rearrange("(j p) c -> p j c", p=P), yb[q][:]).then_inc(out_d, 16)
                        sp.wait_ge(out_d, t(16) + 16)
                        sp.sem_inc(S["stored"], 1)
                stages(sp, node, expert)
                sp.wait_ge(out_d, 16 * NI)

            @block.tensor
            def _(pe):
                ident = K.cst[:, C_ID:C_ID + P]

                def node(k, q, t, before):
                    if k not in (3, 4):
                        return
                    for j in range(IB):
                        f = (k - 3) * IB + j
                        bank = ps_n[f % 2]
                        pe.wait_ge(S["node_reads"], ONE + t(NPR) + (f if j == 0 else f - 1))
                        if k == 3:
                            pe.wait_ge(S["zn_done"], ONE + t(IB) + (j + 1))
                            for kh in range(2):
                                mm = pe.transpose(bank[:, kh * P:(kh + 1) * P], x7[:, j, kh * P:(kh + 1) * P], ident)
                        else:
                            for kh in range(2):
                                mm = pe.matmul(bank[:, 0:E], zt[q][:, kh, j * P:(j + 1) * P], K.wr[:, kh, :], start=(kh == 0), stop=(kh == 1))
                        mm.then_inc(S["node_products"], 1)

                def expert(e, q, t):
                    if e == 0:
                        pe.wait_ge(S["node_reads"], ONE + t(NPR) + NPR)
                    pe.wait_ge(w_in[e], 48)
                    done = t(E * HB) + (e * HB)
                    for layer in range(2):
                        wl, src = ((w1, zt[q]), (w2, h1))[layer]
                        for half in range(2):
                            for mh in range(2):
                                g = layer * 4 + half * 2 + mh
                                pe.wait_ge(S["hidden_done"], ONE + done + (g + 1))
                                if layer == 1 and mh == 0:
                                    pe.wait_ge(S["hidden_done"], ONE + done + (4 + half * 2 + 2))
                                for kh in range(2):
                                    mm = pe.matmul(ps_h[g % 4][:, 0:HN], wl[:, kh, e, mh * P:(mh + 1) * P],
                                                   src[:, kh, half * HN:(half + 1) * HN], start=(kh == 0), stop=(kh == 1))
                                mm.then_inc(S["hidden_products"], 1)
                    for j in range(IB):
                        if j in (0, HN // P):
                            pe.wait_ge(S["hidden_done"], ONE + done + (4 + 6 + (2 if j else 0)))
                        pe.wait_ge(S["expert_added"], ONE + t(E * IB) + (e * IB + max(j - 1, 0)))
                        for kh in range(2):
                            mm = pe.matmul(ps_y[j % 2][:, 0:D], h2[:, kh, j * P:(j + 1) * P], wo[:, kh, e, :],
                                           start=(kh == 0), stop=(kh == 1))
                        mm.then_inc(S["expert_products"], 1)
                stages(pe, node, expert)

            @block.scalar
            def _(act):
                def product(k, j, t):
                    act.wait_ge(S["node_products"], ONE + t(NPR) + ((k - 3) * IB + j + 1))

                def node(k, q, t, before):
                    if k == 0:
                        act.wait_ge(mix_in, t(16) + 16)
                        act.activation(small[:, 2, :].unsqueeze(2), t7[:, :, D + 1:D + 2], ACT.Sqrt).then_inc(S["q_root"], 1)
                    elif k == 3:
                        act.wait_ge(S["var_done_e"], ONE + t(1) + 1)
                        act.activation(small[:, 9, :], small[:, 8, :], ACT.Sqrt).then_inc(S["std_done_e"], 1)
                        for j in range(IB):
                            product(k, j, t)
                            act.copy(zt[q][:, :, j * P:(j + 1) * P], ps_n[((k - 3) * IB + j) % 2][:, 0:D].rearrange("p (k n) -> p k n", n=P)).then_inc(S["node_reads"], 1)
                    elif k == 4:
                        act.wait_ge(S["lg_less"], ONE + t(1) + 1)
                        act.activation(lg[:], lg[:], ACT.Exp).then_inc(S["lg_exp"], 1)

                def expert(e, q, t):
                    done = t(E * HB) + (e * HB)
                    for layer in range(2):
                        for half in range(2):
                            for mh in range(2):
                                g = layer * 4 + half * 2 + mh
                                act.wait_ge(S["hidden_products"], ONE + done + (g + 1))
                                c = 2 * e + mh
                                act.activation((h1, h2)[layer][:, mh, half * HN:(half + 1) * HN], ps_h[g % 4][:, 0:HN],
                                               ACT.Relu, bias=K.bnb[:, layer, c:c + 1], scale=K.bns[:, layer, c:c + 1])\
                                   .then_inc(S["hidden_done"], 1)
                stages(act, node, expert)

            @block.vector
            def _(dve):
                def product(k, j, t):
                    dve.wait_ge(S["node_products"], ONE + t(NPR) + ((k - 3) * IB + j + 1))

                def bank(k, j):
                    return ps_n[((k - 3) * IB + j) % 2]

                def step(name, t, ins):
                    ins.then_inc(S[name], 1)
                    dve.wait_ge(S[name], ONE + t(1) + 1)

                def node(k, q, t, before):
                    at = bass.ds(t(IB), IB)
                    if k == 0:
                        dve.wait_ge(mix_in, t(16) + 16)
                        step("q_small1", t, dve.tensor_scalar(small[:, 3, :].unsqueeze(2), t7[:, :, D:D + 1], DIV_EPS, None, ALU.add))
                        step("q_small2", t, dve.reciprocal(small[:, 4, :], small[:, 3, :]))
                        dve.wait_ge(S["q_root"], ONE + t(1) + 1)
                        step("q_small3", t, dve.tensor_tensor(small[:, 5, :], small[:, 2, :], small[:, 4, :], ALU.mult))
                        step("q_small4", t, dve.tensor_scalar(small[:, 6, :], small[:, 5, :], NORM_EPS, None, ALU.max))
                        step("q_small5", t, dve.reciprocal(small[:, 7, :], small[:, 6, :]))
                        step("q_small6", t, dve.tensor_tensor(small[:, 5, :], small[:, 7, :], small[:, 4, :], ALU.mult))
                    elif k in (1, 2):
                        if k == 1:
                            dve.wait_ge(x_in, t(16) + 16)
                            if before:
                                dve.wait_ge(S["stored"], ONE + before(1))
                            step("den_done", t, dve.reciprocal(den[:].unsqueeze(3), K.acc[:, at, :].rearrange("p j (h c) -> p j h c", c=HC)[:, :, :, HD:HC]))
                        for j in range(HALF) if k == 1 else range(HALF, IB):
                            dve.tensor_tensor(yb[q][:, j, :], t7[:, j, D + 2:MW], x7[:, j, :], ALU.add).then_inc(S["z_based"], 1)
                            dve.scalar_tensor_tensor(t7[:, j, 0:D], t7[:, j, 0:D], small[:, 5, j:j + 1], K.cb[:],
                                                     ALU.mult, ALU.add).then_inc(S["mix_scaled"], 1)
                            a = K.acc[:, bass.ds(t(IB) + j, 1), :]
                            dve.tensor_tensor(q7[:, j, :].rearrange("p (h c) -> p h c", c=HD),
                                              a.rearrange("p o (h c) -> p (o h) c", c=HC)[:, :, 0:HD],
                                              bc(den[:, j, :], 2, HD), ALU.mult).then_inc(S["gat_done"], 1)
                            dve.wait_ge(S["z_based"], ONE + t(IB) + (j + 1))
                            dve.wait_ge(S["mix_scaled"], ONE + t(IB) + (j + 1))
                            dve.tensor_tensor(yb[q][:, j, :], yb[q][:, j, :], t7[:, j, 0:D], ALU.add).then_inc(S["z_const"], 1)
                            dve.wait_ge(S["gat_done"], ONE + t(IB) + (j + 1))
                            dve.wait_ge(S["z_const"], ONE + t(IB) + (j + 1))
                            dve.scalar_tensor_tensor(yb[q][:, j, :], q7[:, j, :], 0.0, yb[q][:, j, :], ALU.max, ALU.add).then_inc(S["z_done"], 1)
                            if j > 0:
                                dve.bn_stats(stats[:, j - 1, :], yb[q][:, j - 1, :]).then_inc(S["stats_done_e"], 1)
                        if k == 1:
                            return
                        dve.wait_ge(S["z_done"], ONE + t(IB) + IB)
                        dve.bn_stats(stats[:, IB - 1, :], yb[q][:, IB - 1, :]).then_inc(S["stats_done_e"], 1)
                        dve.wait_ge(S["stats_done_e"], ONE + t(IB) + IB)
                        settle(dve, S["settled_e"])
                        for j in range(IB):
                            dve.bn_aggr(mv[:, j, :], stats[:, j, :]).then_inc(S["aggr_done_e"], 1)
                        dve.wait_ge(S["aggr_done_e"], ONE + t(IB) + IB)
                        dve.tensor_scalar(small[:, 8, :].unsqueeze(2), mv[:, :, 1:2], LN_EPS, None, ALU.add).then_inc(S["var_done_e"], 1)
                    elif k == 3:
                        dve.wait_ge(S["std_done_e"], ONE + t(1) + 1)
                        step("rstd_done_e", t, dve.reciprocal(small[:, 9, :], small[:, 9, :]))
                        for j in range(IB):
                            dve.tensor_scalar(x7[:, j, :], yb[q][:, j, :], mv[:, j, 0:1], small[:, 9, j:j + 1],
                                              ALU.subtract, ALU.mult).then_inc(S["zn_done"], 1)
                    elif k == 4:
                        for j in range(IB):
                            product(k, j, t)
                            dve.tensor_tensor(lg[:, j, :], bank(k, j)[:, 0:E], K.br[:], ALU.add).then_inc(S["node_reads"], 1)
                        dve.wait_ge(S["node_reads"], ONE + t(NPR) + (k - 2) * IB)
                        step("lg_max", t, dve.tensor_reduce(small[:, 3, :], lg[:], AX, ALU.max))
                        dve.tensor_tensor(lg[:], lg[:], bc(small[:, 3, :], 2, E), ALU.subtract).then_inc(S["lg_less"], 1)
                        dve.wait_ge(S["lg_exp"], ONE + t(1) + 1)
                        step("lg_sum", t, dve.tensor_reduce(small[:, 4, :], lg[:], AX, ALU.add))
                        step("lg_rec", t, dve.reciprocal(small[:, 6, :], small[:, 4, :]))
                        dve.tensor_tensor(wts[q][:], lg[:], bc(small[:, 6, :], 2, E), ALU.mult).then_inc(S["wts_done"], 1)
                    elif k in (5, 6):
                        if k == 5:
                            dve.wait_ge(bo_in, 16)
                            dve.wait_ge(S["wts_done"], ONE + t(1) + 1)
                        dve.wait_ge(S["expert_added"], ONE + t(E * IB) + (k + 1) * IB)
                        for e in range(E // 2) if k == 5 else range(E // 2, E):
                            dve.wait_ge(S["biased"], ONE + t(E * IB) + e * IB)
                            for j in range(IB):
                                dve.scalar_tensor_tensor(yb[q][:, j, :], bo[:, e, :], wts[q][:, j, e:e + 1], yb[q][:, j, :],
                                                         ALU.mult, ALU.add).then_inc(S["biased"], 1)

                def expert(e, q, t):
                    if e == 0:
                        dve.wait_ge(S["z_done"], ONE + t(IB) + IB)
                        dve.wait_ge(S["wts_done"], ONE + t(1) + 1)
                    elif e > 5:
                        dve.wait_ge(S["biased"], ONE + t(E * IB) + (e - 5) * (E // 2) * IB)
                    dve.wait_ge(S["expert_added"], ONE + t(E * IB) + e * IB)
                    for j in range(IB):
                        dve.wait_ge(S["expert_products"], ONE + t(E * IB) + (e * IB + j + 1))
                        dve.scalar_tensor_tensor(yb[q][:, j, :], ps_y[j % 2][:, 0:D], wts[q][:, j, e:e + 1], yb[q][:, j, :],
                                                 ALU.mult, ALU.add).then_inc(S["expert_added"], 1)
                stages(dve, node, expert)


def graph_layer(nc, io):
    with ExitStack() as ctx:
        m = Mem(nc, ctx)
        Mem.sems = []
        dr = {"src": nc.dram_tensor("list_src", [LROWS, GE], I32).ap(),
              "dst": nc.dram_tensor("list_dst", [LROWS, GE], I32).ap(),
              "table": nc.dram_tensor("edge_table", [NPAD, TW], F32).ap(),
              "xnt": nc.dram_tensor("xn_turned", [NS, P, D], F32).ap(),
              "mix": nc.dram_tensor("mix_rows", [NS * P, MW], F32).ap()}

        class K:
            cst = m.sb("cst", [P, C_W])
            cstb = m.sb("cstb", [P, 2 * P], BF16)
            acc = m.sb("acc", [P, NB, RW])
            state = m.sb("state", [P, NB, 2 * HEADS])
            wq, wvo = (m.sb(n, [P, 2, D]) for n in ("wq", "wvo"))
            kvw = m.sb("kvw", [P, 2, D + 1])
            bqc, cb = m.sb("bqc", [P, 2]), m.sb("cb", [P, D])
            bns, bnb = (m.sb(n, [P, 2, 2 * E]) for n in ("bns", "bnb"))
            wr, br = m.sb("wr", [P, 2, E]), m.sb("br", [P, E])
        with ExitStack() as lists:
            ml = Mem(nc, lists)
            K.rel = ml.sb("rel", [P, NVT * CH], BF16)
            K.last = ml.sb("last", [P, NVT * CH], BF16)
            K.ix = ml.sb("ix", [P, NVT * CH], I32)
            K.brk = ml.sb("brk", [P, NVT // SV, HEADS, SV], BF16)
            K.blk = ml.sb("blk", [1, NVT // 4], I32)
            with ExitStack() as early:
                me = Mem(nc, early)
                K.wcat = me.sb("wcat", [P, 2, D + 2 * HEADS])
                K.wk, K.bq, K.bk, K.bvw = me.sb("wk", [P, 2, D]), me.sb("bq", [P, D]), me.sb("bk", [P, D]), me.sb("bvw", [P, D])
                with ExitStack() as given:
                    W = Given(Mem(nc, given), io, K)
                    edge_lists(nc, io, dr, K, W)
                    weights(nc, K, W)
                project(nc, io, dr, K)
            Mem.clear(nc)
            attend(nc, dr, K)
        experts(nc, io, dr, K)


def kernel(**inputs):
    import concourse.bacc as bacc
    from concourse.bass_utils import run_bass_kernel_spmd as run

    a = {k: np.asarray(v) for k, v in inputs.items()}

    def rows(w):
        return np.ascontiguousarray(w.reshape(2, P, -1).transpose(1, 0, 2))

    def expert_rows(w):
        return np.ascontiguousarray(w.reshape(E, 2, P, D).transpose(2, 1, 0, 3))

    def channels(v):
        return v.reshape(E, 2, P).transpose(2, 0, 1).reshape(P, 2 * E)

    def edges(v, fill):
        out = np.full(LROWS * GE, fill, v.dtype)
        out[:EDGES] = v
        return out.reshape(LROWS, GE)

    x = np.zeros((NPAD, D), a["x"].dtype)
    x[:N] = a["x"]
    cst = np.zeros((P, C_W), np.float32)
    cst[:, C_ID:C_ID + P] = np.eye(P)
    cst[:, C_IOTA:C_IOTA + P] = np.arange(P)
    cst[:, C_VALID:C_VALID + NB] = np.arange(NB) * P + np.arange(P)[:, None] < N
    cst[:, C_GLAST] = np.arange(P) % CH == CH - 1
    cst[:, C_THR] = np.arange(P) * P
    cst_row = np.zeros((1, NVT), np.float32)
    cst_row[0, NG:NG + NX] = np.arange(1, NB)
    f = {k: a["L0_ffn_" + k] for k in ("b1", "g1", "be1", "m1", "v1", "b2", "g2", "be2", "m2", "v2")}
    given = {
        "x": x, "src": edges(a["src"], 0), "dst": edges(a["dst"], NODST), "cst": cst, "cst_row": cst_row,
        "firsts": np.ascontiguousarray(a["dst"][::GE].reshape(1, NG)),
        "w_gat": rows(a["L0_gnn_W"]), "att_src": a["L0_gnn_att_src"].reshape(D), "att_dst": a["L0_gnn_att_dst"].reshape(D),
        "w_qkv": rows(a["L0_mix_W_qkv"]), "b_qkv": a["L0_mix_b_qkv"],
        "bv_col": np.ascontiguousarray(a["L0_mix_b_qkv"][2 * D:].reshape(2, P).T),
        "w_out": rows(a["L0_mix_W_out"]), "b_out": a["L0_mix_b_out"],
        "w_r": rows(a["L0_ffn_Wr"]), "b_r": a["L0_ffn_br"], "b_o": a["L0_ffn_bo"],
        "w1": expert_rows(a["L0_ffn_W1"]), "w2": expert_rows(a["L0_ffn_W2"]), "wo": expert_rows(a["L0_ffn_Wo"]),
        "bn": np.stack([channels(f[n + i]) for n in ("b", "g", "be", "m", "v") for i in "12"], axis=1),
    }
    nc = bacc.Bacc("TRN2", target_bir_lowering=False, num_devices=1)
    io = {k: nc.dram_tensor(f"in_{k}", v.shape, mybir.dt.from_np(v.dtype), kind="ExternalInput").ap()
          for k, v in given.items()}
    io["out"] = nc.dram_tensor("out_x", (NPAD, D), F32, kind="ExternalOutput").ap()
    graph_layer(nc, io)
    r = run(nc, [{f"in_{k}": v for k, v in given.items()}], core_ids=[0])
    return r.results[0]["out_x"][:N]
```
